# Optimizing a Trainium2 kernel written in Bass

```python
import numpy as np
import jax
import jax.numpy as jnp

def _softmax(x, axis=-1):
    return jax.nn.softmax(x, axis=axis)

def _gelu(x):
    return jax.nn.gelu(x, approximate=True)

def _silu(x):
    return jax.nn.silu(x)

def _sigmoid(x):
    return jax.nn.sigmoid(x)

def _layernorm(x, axis=-1, eps=1e-05):
    m = jnp.mean(x, axis=axis, keepdims=True)
    v = jnp.var(x, axis=axis, keepdims=True)
    return (x - m) / jnp.sqrt(v + eps)

def _scatter_add(tgt, idx, src, axis=0):
    return tgt.at[idx].add(src)

def _segment_sum(src, seg, n):
    return jax.ops.segment_sum(src, seg, n)
kernel_name = 'mk_flamingo_gated_d1_seqx_r4_59b707'

def setup_inputs(seed: int=0):
    np.random.seed(seed)
    _w = jnp.asarray

    def _rec_inputs():
        import jax
        import jax.numpy as jnp
        _rk = jax.random.key(seed)
        x = -0.0002928 + 1 * jax.random.normal(jax.random.fold_in(_rk, 1), (4, 512, 256), jnp.float32)
        _lenS = 512 - jax.random.randint(jax.random.fold_in(_rk, 7), (4,), 0, max(1, 512 // 4) + 1, jnp.int32)
        _lenS2 = 512 - jax.random.randint(jax.random.fold_in(_rk, 8), (4,), 0, max(1, 512 // 4) + 1, jnp.int32)
        _ctx_1024P = jax.random.normal(jax.random.fold_in(_rk, 11), (4, 16, 256), jnp.float32)
        _ctx_1024c = jax.random.dirichlet(jax.random.fold_in(_rk, 511), 0.3 * jnp.ones((16,), jnp.float32), (4, 512))
        _ctx_1024t = jnp.einsum('bsk,bkd->bsd', _ctx_1024c, _ctx_1024P)
        _ctx_1024t = _ctx_1024t * jax.lax.rsqrt(jnp.mean(jnp.square(_ctx_1024t)) + 1e-12) * 0.953939
        ctx_1024 = -1.39393e-06 + 0.999914 * (_ctx_1024t + 0.3 * jax.random.normal(jax.random.fold_in(_rk, 611), (4, 512, 256), jnp.float32))
        _g = jax.random.normal(jax.random.fold_in(_rk, 9001), (2, 1), jnp.float32)
        _g = jnp.sign(_g) * jnp.maximum(jnp.abs(_g), 1.0) + (_g == 0) * 1.0
        g_xattn = _g[0]
        g_ffn = _g[1]
        return (x, ctx_1024, g_xattn, g_ffn)
    x, ctx_1024, g_xattn, g_ffn = _rec_inputs()

    def _L0_xattn_setup():
        import jax, jax.numpy as jnp
        import numpy as np
        D_MODEL = 256
        NUM_HEADS = 16
        D_HEAD = D_MODEL // NUM_HEADS
        key = jax.random.key(seed)
        ks = jax.random.split(key, 9)
        B, L, E = (2, 512, D_MODEL)
        bound = 1.0 / np.sqrt(E)
        inp = {'query': jax.random.normal(ks[0], (B, L, E), dtype=jnp.float32), 'key': jax.random.normal(ks[1], (B, L, E), dtype=jnp.float32), 'value': jax.random.normal(ks[2], (B, L, E), dtype=jnp.float32), 'wq': jax.random.uniform(ks[3], (E, E), jnp.float32, -bound, bound), 'bq': jax.random.uniform(ks[4], (E,), jnp.float32, -bound, bound), 'wk': jax.random.uniform(ks[5], (E, E), jnp.float32, -bound, bound), 'bk': jax.random.uniform(ks[6], (E,), jnp.float32, -bound, bound), 'wv': jax.random.uniform(ks[7], (E, E), jnp.float32, -bound, bound), 'bv': jax.random.uniform(ks[8], (E,), jnp.float32, -bound, bound)}
        return inp
    _L0_xattn_all = _L0_xattn_setup()
    _L0_xattn_in = {k: v for k, v in _L0_xattn_all.items() if k in ('wq', 'bq', 'wk', 'bk', 'wv', 'bv')}
    del _L0_xattn_all

    def _L0_ffn_setup():
        import jax, jax.numpy as jnp
        import numpy as np
        D = 256
        H = 16
        DH = D // H
        DC = D // 4
        HID = 512
        G = 2
        EPG = 4
        E = G * EPG
        TOPK = 2
        EPS = 1e-06
        B, T = (2, 512)

        def _rope_sincos(t, dh):
            inv_freq = 1.0 / 10000.0 ** (jnp.arange(0, dh, 2, dtype=jnp.float32) / dh)
            ang = jnp.arange(t, dtype=jnp.float32)[:, None] * inv_freq[None, :]
            return (jnp.sin(ang), jnp.cos(ang))

        def _apply_rope(x, sin, cos):
            x1 = x[..., ::2]
            x2 = x[..., 1::2]
            r = jnp.stack([x1 * cos - x2 * sin, x1 * sin + x2 * cos], axis=-1)
            return r.reshape(x.shape)

        def _swiglu(x):
            a, b = jnp.split(x, 2, axis=-1)
            return jax.nn.silu(a) * b

        def _rmsnorm(x, w):
            return x * jax.lax.rsqrt(jnp.mean(x * x, axis=-1, keepdims=True) + EPS) * w
        key = jax.random.key(seed)
        ks = jax.random.split(key, 14)
        s = 0.02
        return {'src': jax.random.normal(ks[0], (B, T, D), jnp.float32), 'Wq': jax.random.normal(ks[1], (D, D), jnp.float32) * s, 'Wk_c': jax.random.normal(ks[2], (D, DC), jnp.float32) * s, 'Wv_c': jax.random.normal(ks[3], (D, DC), jnp.float32) * s, 'Wk': jax.random.normal(ks[4], (DC, D), jnp.float32) * s, 'Wv': jax.random.normal(ks[5], (DC, D), jnp.float32) * s, 'Wo': jax.random.normal(ks[6], (D, D), jnp.float32) * s, 'W_shared_in': jax.random.normal(ks[7], (D, 2 * HID), jnp.float32) * s, 'W_shared_out': jax.random.normal(ks[8], (HID, D), jnp.float32) * s, 'W1_shared': jax.random.normal(ks[9], (D, 2 * HID), jnp.float32) * s, 'W2_experts': jax.random.normal(ks[10], (E, HID, D), jnp.float32) * s, 'Wg_gate': jax.random.normal(ks[11], (D, G), jnp.float32) * s, 'We_gate': jax.random.normal(ks[12], (D, E), jnp.float32) * s, 'group_bias': jnp.zeros((G,), jnp.float32), 'expert_bias': jnp.zeros((E,), jnp.float32), 'norm1_w': jnp.ones((D,), jnp.float32), 'norm2_w': jnp.ones((D,), jnp.float32)}
    _L0_ffn_all = _L0_ffn_setup()
    _L0_ffn_in = {k: v for k, v in _L0_ffn_all.items() if k in ('Wq', 'Wk_c', 'Wv_c', 'Wk', 'Wv', 'Wo', 'W_shared_in', 'W_shared_out', 'W1_shared', 'W2_experts', 'Wg_gate', 'We_gate', 'group_bias', 'expert_bias', 'norm1_w', 'norm2_w')}
    del _L0_ffn_all
    return {'x': x, 'ctx_1024': ctx_1024, 'g_xattn': g_xattn, 'g_ffn': g_ffn, 'L0_xattn_wq': _L0_xattn_in['wq'], 'L0_xattn_bq': _L0_xattn_in['bq'], 'L0_xattn_wk': _L0_xattn_in['wk'], 'L0_xattn_bk': _L0_xattn_in['bk'], 'L0_xattn_wv': _L0_xattn_in['wv'], 'L0_xattn_bv': _L0_xattn_in['bv'], 'L0_ffn_Wq': _L0_ffn_in['Wq'], 'L0_ffn_Wk_c': _L0_ffn_in['Wk_c'], 'L0_ffn_Wv_c': _L0_ffn_in['Wv_c'], 'L0_ffn_Wk': _L0_ffn_in['Wk'], 'L0_ffn_Wv': _L0_ffn_in['Wv'], 'L0_ffn_Wo': _L0_ffn_in['Wo'], 'L0_ffn_W_shared_in': _L0_ffn_in['W_shared_in'], 'L0_ffn_W_shared_out': _L0_ffn_in['W_shared_out'], 'L0_ffn_W1_shared': _L0_ffn_in['W1_shared'], 'L0_ffn_W2_experts': _L0_ffn_in['W2_experts'], 'L0_ffn_Wg_gate': _L0_ffn_in['Wg_gate'], 'L0_ffn_We_gate': _L0_ffn_in['We_gate'], 'L0_ffn_group_bias': _L0_ffn_in['group_bias'], 'L0_ffn_expert_bias': _L0_ffn_in['expert_bias'], 'L0_ffn_norm1_w': _L0_ffn_in['norm1_w'], 'L0_ffn_norm2_w': _L0_ffn_in['norm2_w']}

def reference(x, ctx_1024, g_xattn, g_ffn, L0_xattn_wq, L0_xattn_bq, L0_xattn_wk, L0_xattn_bk, L0_xattn_wv, L0_xattn_bv, L0_ffn_Wq, L0_ffn_Wk_c, L0_ffn_Wv_c, L0_ffn_Wk, L0_ffn_Wv, L0_ffn_Wo, L0_ffn_W_shared_in, L0_ffn_W_shared_out, L0_ffn_W1_shared, L0_ffn_W2_experts, L0_ffn_Wg_gate, L0_ffn_We_gate, L0_ffn_group_bias, L0_ffn_expert_bias, L0_ffn_norm1_w, L0_ffn_norm2_w):
    import jax
    import jax.numpy as jnp

    def _L0_xattn_ref(query, key, value, wq, bq, wk, bk, wv, bv):
        import jax, jax.numpy as jnp
        import numpy as np
        D_MODEL = 256
        NUM_HEADS = 16
        D_HEAD = D_MODEL // NUM_HEADS
        B, L, E = query.shape
        H, Dh = (NUM_HEADS, D_HEAD)
        scale = Dh ** 0.5
        q = (query @ wq.T + bq).reshape(B, L, H, Dh).transpose(0, 2, 1, 3)
        k = (key @ wk.T + bk).reshape(B, L, H, Dh).transpose(0, 2, 1, 3)
        v = (value @ wv.T + bv).reshape(B, L, H, Dh).transpose(0, 2, 1, 3)
        scores = jnp.einsum('bhld,bhsd->bhls', q, k) / scale
        attn = jax.nn.softmax(scores, axis=-1)
        out = jnp.einsum('bhls,bhsd->bhld', attn, v)
        return out.transpose(0, 2, 1, 3).reshape(B, L, E)

    def _L0_ffn_ref(src, Wq, Wk_c, Wv_c, Wk, Wv, Wo, W_shared_in, W_shared_out, W1_shared, W2_experts, Wg_gate, We_gate, group_bias, expert_bias, norm1_w, norm2_w):
        import jax, jax.numpy as jnp
        import numpy as np
        D = 256
        H = 16
        DH = D // H
        DC = D // 4
        HID = 512
        G = 2
        EPG = 4
        E = G * EPG
        TOPK = 2
        EPS = 1e-06
        B, T = (2, 512)

        def _rope_sincos(t, dh):
            inv_freq = 1.0 / 10000.0 ** (jnp.arange(0, dh, 2, dtype=jnp.float32) / dh)
            ang = jnp.arange(t, dtype=jnp.float32)[:, None] * inv_freq[None, :]
            return (jnp.sin(ang), jnp.cos(ang))

        def _apply_rope(x, sin, cos):
            x1 = x[..., ::2]
            x2 = x[..., 1::2]
            r = jnp.stack([x1 * cos - x2 * sin, x1 * sin + x2 * cos], axis=-1)
            return r.reshape(x.shape)

        def _swiglu(x):
            a, b = jnp.split(x, 2, axis=-1)
            return jax.nn.silu(a) * b

        def _rmsnorm(x, w):
            return x * jax.lax.rsqrt(jnp.mean(x * x, axis=-1, keepdims=True) + EPS) * w
        Bb, Tt, C = src.shape
        q = (src @ Wq).reshape(Bb, Tt, H, DH).transpose(0, 2, 1, 3)
        k = (src @ Wk_c @ Wk).reshape(Bb, Tt, H, DH).transpose(0, 2, 1, 3)
        v = (src @ Wv_c @ Wv).reshape(Bb, Tt, H, DH).transpose(0, 2, 1, 3)
        sin, cos = _rope_sincos(Tt, DH)
        q = _apply_rope(q, sin, cos)
        k = _apply_rope(k, sin, cos)
        attn = jnp.einsum('bhqd,bhkd->bhqk', q, k) / np.sqrt(DH).astype(np.float32)
        attn = jax.nn.softmax(attn, axis=-1)
        sa = jnp.einsum('bhqk,bhkd->bhqd', attn, v)
        sa = sa.transpose(0, 2, 1, 3).reshape(Bb, Tt, C) @ Wo
        x = _rmsnorm(src + sa, norm1_w)
        S = Bb * Tt
        flat = x.reshape(S, C)
        shared = _swiglu(flat @ W_shared_in) @ W_shared_out
        g_probs = jax.nn.softmax(flat @ Wg_gate + group_bias, -1)
        g_idx = jnp.argmax(g_probs, axis=-1)
        e_logits = flat @ We_gate + expert_bias
        e_group = jnp.arange(E) // EPG
        in_group = e_group[None, :] == g_idx[:, None]
        e_probs = jax.nn.softmax(jnp.where(in_group, e_logits, -jnp.inf), -1)
        g_prob = jnp.take_along_axis(g_probs, g_idx[:, None], axis=1)
        p_expert = e_probs * g_prob
        topv, topi = jax.lax.top_k(p_expert, TOPK)
        w = jnp.zeros((S, E), flat.dtype).at[jnp.arange(S)[:, None], topi].set(topv)
        h = _swiglu(flat @ W1_shared)
        routed = jnp.zeros_like(shared)
        for e in range(E):
            routed = routed + h @ W2_experts[e] * w[:, e:e + 1]
        out = x + (shared + routed).reshape(Bb, Tt, C)
        return _rmsnorm(out, norm2_w)
    x = x + jnp.tanh(g_xattn[0]) * _L0_xattn_ref(_layernorm(x, axis=-1), ctx_1024, ctx_1024, L0_xattn_wq, L0_xattn_bq, L0_xattn_wk, L0_xattn_bk, L0_xattn_wv, L0_xattn_bv)
    x = x + jnp.tanh(g_ffn[0]) * _L0_ffn_ref(_layernorm(x, axis=-1), L0_ffn_Wq, L0_ffn_Wk_c, L0_ffn_Wv_c, L0_ffn_Wk, L0_ffn_Wv, L0_ffn_Wo, L0_ffn_W_shared_in, L0_ffn_W_shared_out, L0_ffn_W1_shared, L0_ffn_W2_experts, L0_ffn_Wg_gate, L0_ffn_We_gate, L0_ffn_group_bias, L0_ffn_expert_bias, L0_ffn_norm1_w, L0_ffn_norm2_w)
    return x

_drawn_inputs = setup_inputs


def setup_inputs(seed=0):
    import zlib

    import numpy as np

    out = dict(_drawn_inputs(seed))
    spreads = {'L0_ffn_group_bias': (0.0, 2.0),
     'L0_ffn_expert_bias': (0.0, 2.0),
     'L0_ffn_norm1_w': (1.0, 0.2),
     'L0_ffn_norm2_w': (1.0, 0.2)}
    factors = {'L0_xattn_bq': 8.0,
     'L0_xattn_bk': 200.0,
     'L0_ffn_Wq': 8.0,
     'L0_ffn_Wk_c': 8.0,
     'L0_ffn_Wv_c': 4.759,
     'L0_ffn_Wk': 8.0,
     'L0_ffn_Wv': 4.464,
     'L0_ffn_Wo': 4.527,
     'L0_ffn_Wg_gate': 19.846,
     'L0_ffn_We_gate': 21.341,
     'L0_ffn_W1_shared': 4.05,
     'L0_ffn_W2_experts': 4.05,
     'L0_ffn_W_shared_in': 5.25,
     'L0_ffn_W_shared_out': 5.272}
    for name, (base, spread) in spreads.items():
        noise = np.random.default_rng([zlib.crc32(name.encode()), seed]).standard_normal(out[name].shape)
        drawn = base * np.exp(spread * noise) if base else spread * noise
        out[name] = jnp.asarray(drawn.astype(out[name].dtype))
    for name, factor in factors.items():
        out[name] = (out[name] * factor).astype(out[name].dtype)
    return out
```

```python
from contextlib import ExitStack

import numpy as np
import concourse.bass as bass
from concourse import mybir

F32 = mybir.dt.float32
BF16 = mybir.dt.bfloat16
I32 = mybir.dt.int32
ALU = mybir.AluOpType
ACT = mybir.ActivationFunctionType
AX = mybir.AxisListType

P = 128
HG = 4
NTERM = 6
NPART = 3
Q_PART = [0, 0, 0, 1, 1, 2]
K_PART = [0, 1, 2, 0, 1, 0]
LEAD = 12
PROB_SLOTS = 3
MISC_BANKS = [7, 0, 1]


def flamingo_block(nc, x, ctx_in, g_xattn, g_ffn, wq, bq, wk, bk, wv, bv,
                   f_wq, f_wkc, f_wvc, f_wk, f_wv, f_wo, f_in, f_out, f_w1, f_w2,
                   f_gg, f_ge, f_gb, f_eb, n1, n2, rope, out):
    B, L, D = x.shape
    NH = 16
    DH = D // NH
    TT = L // P
    CT = D // P
    NG = NH // HG
    HID = f_out.shape[0]
    HT = HID // P
    NE = f_w2.shape[0]
    NGRP = f_gg.shape[1]
    EPG = NE // NGRP
    NR = NGRP + NE
    DC = f_wkc.shape[1]
    STK = NTERM * DH
    KROWS = STK + NPART
    NI = 4
    PAIRS = NH * TT // 2
    UNITS = NH * TT
    KTS = NG * TT
    STEPS = UNITS // NG
    SC = 1.0 / float(DH) ** 0.5
    assert (L, D, DH, CT, TT, DC, EPG) == (512, 256, 16, 2, 4, 64, 4)

    P1_TILES, P2_TILES, F_TILES = 10, 9, 7 + 2 * 2 * HT + 2 + TT * NE // 2
    N_MISC = 2 * (P1_TILES + P2_TILES + F_TILES)
    N_X7 = 2 * NI * NG
    HOOKS = {(0, 0, 9): [("p1", 1)], (1, 0, 15): [("p2", 0)], (2, 0, 15): [("p2", 1)], (3, 0, 15): [("f", 0)]}
    VM = DH + 1

    es = ExitStack()
    with es:
        def sb(name, shape, dt):
            return es.enter_context(nc.sbuf_tensor(name, shape, dt))

        def sem(name):
            return es.enter_context(nc.semaphore(name))

        wT = sb("wT", [P, 3, CT, D], F32)
        fq = sb("fq", [P, CT, D], F32)
        fkvc = sb("fkvc", [P, CT, 2 * DC], F32)
        fkv = sb("fkv", [P, D], F32)
        fo = sb("fo", [P, CT, D], F32)
        fin = sb("fin", [P, 2, CT, 2 * HID], F32)
        fout = sb("fout", [P, HT, D], F32)
        w2 = sb("w2", [P, HT, NE, D], F32)
        fg = sb("fg", [P, CT, NR], F32)
        bqk = sb("bqk", [P, 2, CT], F32)
        bv_bc = sb("bv_bc", [P, D], F32)
        n1_bc = sb("n1_bc", [P, D], F32)
        n2_bc = sb("n2_bc", [P, D], F32)
        gb_bc = sb("gb_bc", [P, NR], F32)
        gates = sb("gates", [P, 2], F32)
        tg = sb("tg", [P, 2], F32)
        rope_sb = sb("rope_sb", [P, 2, L], F32)
        identf = sb("identf", [P, P], F32)
        identb = sb("identb", [P, P], BF16)
        rank0 = sb("rank0", [P, TT, NGRP, EPG], F32)
        xin = [sb(f"xin{i}", [P, TT, D], F32) for i in range(2)]
        ctxs = sb("ctxs", [P, TT, D], F32)
        src = [sb(f"src{i}", [P, TT, D], F32) for i in range(2)]
        sa = [sb(f"sa{i}", [P, TT, D], F32) for i in range(2)]
        nT = sb("nT", [P, CT, L], F32)
        cT = sb("cT", [P, CT, L], F32)
        qk = [sb(f"qk{i}", [P, 2, L], F32) for i in range(2)]
        hT = sb("hT", [P, HT, L], F32)
        rb = [hT[:, 2 * X:2 * X + 2, :] for X in range(2)]
        parts = [sb(f"parts{i}", [P, NPART, 2, L], BF16) for i in range(2)]
        qs = sb("qs", [KROWS, NG, HG, L], BF16)
        ks = sb("ks", [KROWS, NG, HG, L], BF16)
        vp = [sb(f"vp{i}", [P, TT, NH, VM], F32) for i in range(2)]
        prob = sb("prob", [P, PROB_SLOTS, HG, L], F32)
        oT = sb("oT", [P, L], F32)
        negm = sb("negm", [P, 2, TT, HG], F32)
        mres = sb("mres", [P, 2, TT, HG], F32)
        m3 = sb("m3", [P, 2, TT, NPART, HG], BF16)
        mTs = sb("mTs", [NPART * HG, 2, L], BF16)
        rec = sb("rec", [P, TT, HG], F32)
        bst = sb("bst", [P, TT, 6], F32)
        mean = sb("mean", [P, TT], F32)
        mdif = sb("mdif", [P, TT], F32)
        nv = sb("nv", [P, TT], F32)
        ny = sb("ny", [P, TT], F32)
        nt_ = sb("nt", [P, TT], F32)
        th = qk[0]
        uu = ctxs[:].rearrange("p (j t) c -> p j (t c)", j=2)
        lg = sb("lg", [P, TT, NR], F32)
        gmx = sb("gmx", [P, TT, 1], F32)
        emx = sb("emx", [P, TT, NGRP], F32)
        zr = sb("zr", [P, TT, NR], F32)
        ez = sb("ez", [P, TT, NR], F32)
        gsum = sb("gsum", [P, TT, 1], F32)
        gtop = sb("gtop", [P, TT, 1], F32)
        esum = sb("esum", [P, TT, NGRP], F32)
        gsel = sb("gsel", [P, TT, NGRP], F32)
        rank = sb("rank", [P, TT, NGRP, EPG], F32)
        cmp = sb("cmp", [P, TT, NGRP, EPG], F32)
        we = sb("we", [P, TT, NGRP, EPG], F32)

        ps = es.enter_context(nc.psum_tensor("ps", [P, 8, L], F32))
        scr = nc.dram_tensor("scr", [2, 2, NPART, D, L], BF16, kind="Internal").ap()

        s_w = sem("weights_loaded")
        s_wn = sem("xattn_weights_loaded")
        s_id = sem("identity_steps")
        s_wt = sem("weight_transposed")
        s_wtd = sem("weight_copied")
        s_set = sem("setup_done")
        s_tg = sem("gate_tanh")
        s_ldx = [sem(f"x_loaded{i}") for i in range(2)]
        s_ldc = sem("ctx_loaded")
        s_src = sem("normed_ready")
        s_mt = sem("misc_full")
        s_mf = sem("misc_free")
        s_x7 = sem("turned_full")
        s_x7f = sem("turned_free")
        s_qk = sem("qk_ready")
        s_spl = sem("parts_ready")
        s_pool = sem("pool_chain")
        s_scr = [sem(f"scratch_written{i}") for i in range(2)]
        s_stk = [sem(f"stack_loaded{g}") for g in range(NG)]
        s_vp = sem("values_ready")
        s_sS = sem("max_tile_full")
        s_sF = sem("max_tile_free")
        s_m3 = sem("maximum_parts")
        s_mts = sem("maximum_turned")
        s_mrow = sem("maximum_rows")
        s_sT = sem("score_full")
        s_exp = sem("exp_done")
        s_pv = sem("value_product")
        s_oc = sem("value_copied")
        s_sa = sem("self_attention_ready")
        s_th = sem("tanh_ready")
        s_xr = sem("block_normed")
        s_zr = sem("router_shifted")
        s_ez = sem("router_exp")
        s_fin = sem("result_ready")
        s_st = sem("result_stored")
        s_dve = sem("dve_chain")
        s_held = sem("waits_passed")

        def hold(eng, s_, value):
            eng.wait_ge(s_, value)
            eng.sem_inc(s_held, 1)

        block = es.enter_context(nc.Block())

        def stages_at(l, g, s):
            return HOOKS.get((l, g, s), [])

        class Turns:
            n = 0

            def take(self):
                self.n += 1
                return self.n - 1

        @block.sync
        def _(sp):
            for s_, d_ in ((src[0], wq), (src[1], wk), (sa[0], wv)):
                sp.dma_start(s_[:, 0:CT, :], d_.rearrange("(o p) c -> p o c", p=P)).then_inc(s_wn, 16)
            n = 0
            for d_, s_ in (
                (bqk[:, 0, :], bq.rearrange("(o p) -> p o", p=P)),
                (bqk[:, 1, :], bk.rearrange("(o p) -> p o", p=P)),
                (bv_bc[:], bv.unsqueeze(0).to_broadcast([P, D])),
                (n1_bc[:], n1.unsqueeze(0).to_broadcast([P, D])),
                (n2_bc[:], n2.unsqueeze(0).to_broadcast([P, D])),
                (gb_bc[:, 0:NGRP], f_gb.unsqueeze(0).to_broadcast([P, NGRP])),
                (gb_bc[:, NGRP:NR], f_eb.unsqueeze(0).to_broadcast([P, NE])),
                (gates[:, 0:1], g_xattn.unsqueeze(0).to_broadcast([P, 1])),
                (gates[:, 1:2], g_ffn.unsqueeze(0).to_broadcast([P, 1])),
                (rope_sb[:], rope.rearrange("s p t -> p s t")),
                (hT[:, 0, :].rearrange("p (k n) -> p k n", k=CT), f_wq.rearrange("(k p) n -> p k n", p=P)),
                (fkvc[:, :, 0:DC], f_wkc.rearrange("(k p) n -> p k n", p=P)),
                (fkvc[:, :, DC:2 * DC], f_wvc.rearrange("(k p) n -> p k n", p=P)),
                (hT[0:DC, 1, 0:D], f_wk),
                (fkv[DC:2 * DC, :], f_wv),
                (fo[:], f_wo.rearrange("(k p) n -> p k n", p=P)),
                (fg[:, :, 0:NGRP], f_gg.rearrange("(k p) n -> p k n", p=P)),
                (fg[:, :, NGRP:NR], f_ge.rearrange("(k p) n -> p k n", p=P)),
                (fin[:, 0], f_in.rearrange("(k p) n -> p k n", p=P)),
                (fin[:, 1], f_w1.rearrange("(k p) n -> p k n", p=P)),
                (fout[:], f_out.rearrange("(k p) n -> p k n", p=P)),
            ):
                sp.dma_start(d_, s_, allow_slow_non_contiguous=True).then_inc(s_w, 16)
                n += 1
            for e in range(NE):
                sp.dma_start(w2[:, :, e, :], f_w2[e].rearrange("(k p) n -> p k n", p=P)).then_inc(s_w, 16)
                n += 1
            assert n == N_W
            sp.wait_ge(s_set, 2)

            def stack(i, l):
                par = l % 2
                for g in range(NG):
                    hold(sp, s_stk[g], i * NI * 192 + max(l - 1, 0) * 192)
                for X in range(2):
                    hold(sp, s_spl, i * 2 * NI + 2 * l + X + 1)
                    sp.dma_start(scr[par, X].rearrange("s (o p) t -> p s o t", p=P), parts[X][:]).then_inc(s_scr[X], 16)
                for X in range(2):
                    hold(sp, s_scr[X], i * 16 * NI + 16 * (l + 1))
                for g in range(NG):
                    if l == 0:
                        hold(sp, s_sT, i * NI * UNITS)
                    else:
                        hold(sp, s_sT, i * NI * UNITS + (l - 1) * UNITS + (g + 1) * STEPS)
                    for r in range(NTERM):
                        for X, (dst, which) in enumerate(((qs, Q_PART), (ks, K_PART))):
                            s_ = scr[par, X, which[r]]
                            if l < 2:
                                s_ = s_.rearrange("(h d) t -> d h t", d=DH)
                            else:
                                s_ = s_.rearrange("(d h) t -> d h t", d=DH)
                            sp.dma_start(dst[r * DH:(r + 1) * DH, g, :, :], s_[:, g * HG:(g + 1) * HG, :]).then_inc(s_stk[g], 16)

            with sp.Fori(0, B // 2) as i:
                for a in range(2):
                    hold(sp, s_fin, i * 2)
                    sp.dma_start(xin[a][:], x[bass.ds(i * 2 + a, 1)].rearrange("b (t p) c -> p (b t) c", p=P)).then_inc(s_ldx[a], 16)
                    hold(sp, s_mf, i * N_MISC + (4 if a else 0))
                    if a == 0:
                        sp.dma_start(ctxs[:], ctx_in[bass.ds(i * 2 + a, 1)].rearrange("b (t p) c -> p (b t) c", p=P)).then_inc(s_ldc, 16)
                    else:
                        sp.dma_start(ctxs[:], ctx_in[bass.ds(i * 2 + a, 1)].rearrange("b (t p) c -> p (b t) c", p=P)).then_inc(s_ldc, 16)
                for l in range(NI):
                    stack(i, l)
                for a in range(2):
                    hold(sp, s_fin, i * 2 + a + 1)
                    sp.dma_start(out[bass.ds(i * 2 + a, 1)].rearrange("b (t p) c -> p (b t) c", p=P), sa[a][:]).then_inc(s_st, 16)
            sp.wait_ge(s_st, 16 * B)

        @block.gpsimd
        def _(pool):
            k = [0]

            def link(ins, base=0):
                k[0] += 1
                ins.then_inc(s_pool, 1)
                hold(pool, s_pool, base + k[0])

            pool.memset(identf[:], 0.0).then_inc(s_id, 1)
            pool.memset(identb[:], 0.0).then_inc(s_id, 1)
            pool.wait_ge(s_id, 2)
            for m in (identf, identb):
                pool.affine_select(out=m[:], in_=m[:], compare_op=ALU.not_equal, fill=1.0, base=0,
                                   pattern=[[-1, P]], channel_multiplier=1).then_inc(s_id, 1)

            per = 2 * (2 * 4 + 2 * 5)
            with pool.Fori(0, B // 2) as i:
                k[0] = 0
                for l in range(NI):
                    for X in range(2):
                        hold(pool, s_qk, i * 2 * NI + 2 * l + X + 1)
                        if l >= 2:
                            link(pool.tensor_tensor(qk[X][:], qk[X][:], rb[X], ALU.add), i * per)
                        hold(pool, s_scr[X], i * 16 * NI + 16 * l)
                        link(pool.tensor_scalar(parts[X][:, 0], qk[X][:], 1.0, None, ALU.mult), i * per)
                        link(pool.tensor_tensor(qk[X][:], qk[X][:], parts[X][:, 0], ALU.subtract), i * per)
                        link(pool.tensor_scalar(parts[X][:, 1], qk[X][:], 1.0, None, ALU.mult), i * per)
                        k[0] += 1
                        pool.tensor_tensor(parts[X][:, 2], qk[X][:], parts[X][:, 1], ALU.subtract).then_inc(s_pool, 1)
                        pool.wait_ge(s_pool, i * per + k[0])
                        pool.sem_inc(s_spl, 1)
                assert k[0] == per

        @block.scalar
        def _(act):
            act.wait_ge(s_w, 16 * N_W)
            nc.scalar.activation(tg[:], gates[:], ACT.Tanh).then_inc(s_tg, 1)

            def copy_values(i, gi):
                act.wait_ge(s_pv, i * NI * KTS + TT * (gi + 1))
                act.wait_ge(s_x7, i * N_X7 + turned_before_o(gi))
                nc.scalar.activation(oT[:], ps[:, 6, :], ACT.Copy).then_inc(s_oc, 1)

            def max_rows(i, gi):
                act.wait_ge(s_mts, i * NI * NG + gi + 1)
                for t in range(NPART):
                    act.dma_start(qs[STK + t:STK + t + 1, gi % NG, :, :],
                                  mTs[t * HG:(t + 1) * HG, gi % 2, :]).then_inc(s_mrow, 16)

            def ffn(i, a, base):
                act.wait_ge(s_spl, i * 2 * NI + 2 * NI)
                act.wait_ge(s_zr, i * 2 + a + 1)
                nc.scalar.activation(ez[:], zr[:], ACT.Exp).then_inc(s_ez, 1)
                for net in range(2):
                    for j in range(HT):
                        t = base + 7 + net * (2 * HT + 2) + 2 * j
                        act.wait_ge(s_mt, i * N_MISC + t + 1)
                        nth = net * HT + j
                        if nth >= 2:
                            tp = t - 4 if j >= 2 else t - 6
                            act.wait_ge(s_mf, i * N_MISC + tp + 1)
                        nc.scalar.activation(th[:, nth % 2, :], ps[:, MISC_BANKS[(t - base) % 3], :],
                                             ACT.Tanh, scale=0.5).then_inc(s_th, 1)

            with act.Fori(0, B // 2) as i:
                act.wait_ge(s_pv, i * NI * KTS)
                act.wait_ge(s_mf, i * N_MISC)
                max_rows(i, 0)
                for l in range(NI):
                    for g in range(NG):
                        gi = l * NG + g
                        for s in range(STEPS):
                            u = gi * STEPS + s
                            kt = gi * TT + s // HG
                            act.wait_ge(s_sT, i * NI * UNITS + u + 1)
                            if s % HG == 0 and kt >= PROB_SLOTS:
                                act.wait_ge(s_pv, i * NI * KTS + kt - PROB_SLOTS + 1)
                            nc.scalar.activation(prob[:, kt % PROB_SLOTS, s % HG, :], ps[:, u % 2, :],
                                                 ACT.Exp, scale=SC).then_inc(s_exp, 1)
                            if s == 4 and gi > 0:
                                copy_values(i, gi - 1)
                            if s == 13 and gi + 1 < NI * NG:
                                max_rows(i, gi + 1)
                            for kind, a in stages_at(l, g, s):
                                if kind == "f":
                                    ffn(i, a, BASE[("f", a)])
                copy_values(i, NI * NG - 1)
                ffn(i, 1, BASE[("f", 1)])

        @block.vector
        def _(dve):
            k = [0]
            it = [0]

            def link(ins):
                k[0] += 1
                ins.then_inc(s_dve, 1)
                dve.wait_ge(s_dve, it[0] + k[0])

            def mark(ins):
                k[0] += 1
                ins.then_inc(s_dve, 1)
                return k[0]

            def until(n):
                dve.wait_ge(s_dve, it[0] + n)

            V = nc.vector
            V.memset(ps[:, 6, :], 0.0).then_inc(s_set, 1)
            V.memset(ks[STK:KROWS], 1.0).then_inc(s_dve, 1)
            V.memset(vp[0][:, :, :, DH:VM], 1.0).then_inc(s_dve, 1)
            V.memset(vp[1][:, :, :, DH:VM], 1.0).then_inc(s_dve, 1)
            for e in range(EPG):
                V.memset(rank0[:, :, :, e:e + 1], float(e)).then_inc(s_dve, 1)
            for j in range(3):
                dve.wait_ge(s_wt, j + 1)
                V.tensor_copy(wT[:, j], ps[:, j, :].rearrange("p (c n) -> p c n", c=CT)).then_inc(s_wtd, 1)
            dve.wait_ge(s_wtd, 3)
            dve.wait_ge(s_w, 16 * N_W)
            dve.wait_ge(s_tg, 1)
            V.tensor_scalar(n2_bc[:], n2_bc[:], tg[:, 1:2], None, ALU.mult).then_inc(s_dve, 1)
            for w_, raw in [(fq[:, c_, :], hT[:, 0, c_ * D:(c_ + 1) * D]) for c_ in range(CT)] + [(fkv[0:DC, :], hT[0:DC, 1, 0:D])]:
                for f in range(2):
                    V.tensor_copy(w_[:, f * P:(f + 1) * P].rearrange("p (j h) -> p j h", h=NH),
                                  raw.rearrange("p (h j f) -> p f j h", f=2, j=DH // 2)[:, f]).then_inc(s_dve, 1)
            SETUP = 14
            dve.wait_ge(s_dve, SETUP)
            dve.sem_inc(s_set, 1)

            def rsqrt():
                link(V.tensor_scalar(nt_[:].bitcast(I32), nv[:].bitcast(I32), 1, None, ALU.arith_shift_right))
                link(V.tensor_scalar(ny[:].bitcast(I32), nt_[:].bitcast(I32), -1.0, float(0x5f3759df), ALU.mult, ALU.add))
                for _ in range(4):
                    link(V.tensor_tensor(nt_[:], ny[:], nv[:], ALU.mult))
                    link(V.scalar_tensor_tensor(out=nt_[:], in0=nt_[:], scalar=-0.5, in1=ny[:], op0=ALU.mult, op1=ALU.mult))
                    link(V.scalar_tensor_tensor(out=ny[:], in0=nt_[:], scalar=1.5, in1=ny[:], op0=ALU.add, op1=ALU.mult))

            def moments(t):
                for tt in range(TT):
                    mark(V.bn_stats(bst[:, tt, :], t[:, tt, :]))
                until(k[0])
                mark(V.tensor_tensor(mean[:], bst[:, :, 1], bst[:, :, 4], ALU.add))
                mark(V.tensor_tensor(mdif[:], bst[:, :, 1], bst[:, :, 4], ALU.subtract))
                link(V.tensor_tensor(nv[:], bst[:, :, 2], bst[:, :, 5], ALU.add))
                mark(V.scalar_tensor_tensor(out=mdif[:], in0=mdif[:], scalar=0.25, in1=mdif[:], op0=ALU.mult, op1=ALU.mult))
                link(V.tensor_scalar(mean[:], mean[:], 0.5, None, ALU.mult))
                link(V.scalar_tensor_tensor(out=nv[:], in0=nv[:], scalar=1.0 / D, in1=mdif[:], op0=ALU.mult, op1=ALU.add))

            def layernorm(t, dst):
                moments(t)
                link(V.tensor_scalar(nv[:], nv[:], 1e-5, None, ALU.add))
                rsqrt()
                for tt in range(TT):
                    mark(V.tensor_scalar(dst[:, tt, :], t[:, tt, :], mean[:, tt:tt + 1], ny[:, tt:tt + 1],
                                         ALU.subtract, ALU.mult))
                until(k[0])

            def mean_square_rsqrt(t):
                moments(t)
                link(V.tensor_tensor(mean[:], mean[:], mean[:], ALU.mult))
                link(V.scalar_tensor_tensor(out=nv[:], in0=nv[:], scalar=1e-6, in1=mean[:], op0=ALU.add, op1=ALU.add))
                rsqrt()

            def ready(s):
                until(k[0])
                dve.sem_inc(s, 1)

            class Tiles:
                def __init__(self, i, base):
                    self.i, self.base, self.j = i, base, 0

                def next(self):
                    dve.wait_ge(s_mt, self.i * N_MISC + self.base + self.j + 1)
                    self.j += 1
                    return ps[:, MISC_BANKS[(self.j - 1) % 3], :]

            def free(ins):
                ins.then_inc(s_mf, 1)

            def stage_p1(i, a):
                base = BASE[("p1", a)]
                T = Tiles(i, base)
                for dst in (nT, cT):
                    for c in range(CT):
                        free(V.tensor_copy(dst[:, c, :], T.next()))
                for X in range(2):
                    dve.wait_ge(s_spl, i * 2 * NI + (2 * (a - 1) + X + 1 if a else 0))
                    for o in range(CT):
                        free(V.tensor_scalar(qk[X][:, o, :], T.next(), bqk[:, X, o:o + 1], None, ALU.add))
                    dve.wait_ge(s_mf, i * N_MISC + base + T.j)
                    dve.sem_inc(s_qk, 1)
                dve.wait_ge(s_pv, i * NI * KTS)
                for h in range(TT // 2):
                    v = T.next().rearrange("p (t h d) -> p t h d", t=2, h=NH)
                    for t in range(2):
                        ins = V.tensor_tensor(vp[a][:, 2 * h + t, :, 0:DH], v[:, t],
                                              bv_bc[:].rearrange("p (h d) -> p h d", h=NH), ALU.add)
                        if t:
                            free(ins)
                        else:
                            mark(ins)
                dve.wait_ge(s_mf, i * N_MISC + base + T.j)
                until(k[0])
                dve.sem_inc(s_vp, 1)

            def stage_p2(i, a):
                base = BASE[("p2", a)]
                T = Tiles(i, base)
                l = 2 + a
                for c in range(CT):
                    free(V.tensor_copy(nT[:, c, :], T.next()))

                def rotate(X):
                    dve.wait_ge(s_spl, i * 2 * NI + 2 * (l - 1) + X + 1)
                    e = T.next()
                    mark(V.tensor_tensor(qk[X][:, 0, :], e, rope_sb[:, 0, :], ALU.mult))
                    free(V.tensor_tensor(qk[X][:, 1, :], e, rope_sb[:, 1, :], ALU.mult))
                    o = T.next()
                    mark(V.scalar_tensor_tensor(out=rb[X][:, 0, :], in0=o, scalar=-1.0, in1=rope_sb[:, 1, :],
                                                op0=ALU.mult, op1=ALU.mult))
                    free(V.tensor_tensor(rb[X][:, 1, :], o, rope_sb[:, 0, :], ALU.mult))
                    until(k[0])
                    dve.wait_ge(s_mf, i * N_MISC + base + T.j)
                    dve.sem_inc(s_qk, 1)

                rotate(0)
                free(V.tensor_copy(cT[:, 0, :], T.next()))
                rotate(1)
                dve.wait_ge(s_pv, i * NI * KTS + (l - 1) * KTS)
                for h in range(TT // 2):
                    v = T.next().rearrange("p (t h d) -> p t h d", t=2, h=NH)
                    free(V.tensor_copy(vp[a][:, 2 * h:2 * h + 2, :, 0:DH], v))
                dve.wait_ge(s_mf, i * N_MISC + base + T.j)
                dve.sem_inc(s_vp, 1)

            def route(i, a, logits):
                free(V.tensor_tensor(lg[:], logits, gb_bc[:].unsqueeze(1).to_broadcast([P, TT, NR]), ALU.add))
                dve.wait_ge(s_mf, i * N_MISC + BASE[("f", a)] + 7)
                el = lg[:, :, NGRP:NR].rearrange("p t (g e) -> p t g e", g=NGRP)
                mark(V.tensor_tensor(gmx[:], lg[:, :, 0:1], lg[:, :, 1:2], ALU.max))
                link(V.tensor_reduce(emx[:], el, AX.X, ALU.max))
                mark(V.tensor_tensor(zr[:, :, 0:NGRP], lg[:, :, 0:NGRP], gmx[:].to_broadcast([P, TT, NGRP]), ALU.subtract))
                mark(V.tensor_tensor(zr[:, :, NGRP:NR].rearrange("p t (g e) -> p t g e", g=NGRP), el,
                                     emx[:].unsqueeze(3).to_broadcast([P, TT, NGRP, EPG]), ALU.subtract))
                ready(s_zr)
                dve.wait_ge(s_ez, i * 2 + a + 1)
                ee = ez[:, :, NGRP:NR].rearrange("p t (g e) -> p t g e", g=NGRP)
                mark(V.tensor_reduce(esum[:], ee, AX.X, ALU.add))
                mark(V.tensor_tensor(gsum[:], ez[:, :, 0:1], ez[:, :, 1:2], ALU.add))
                mark(V.tensor_tensor(gtop[:], ez[:, :, 0:1], ez[:, :, 1:2], ALU.max))
                mark(V.tensor_tensor(gsel[:, :, 1:2], ez[:, :, 1:2], ez[:, :, 0:1], ALU.is_gt))
                link(V.tensor_copy(rank[:], rank0[:]))
                mark(V.reciprocal(esum[:], esum[:]))
                mark(V.reciprocal(gsum[:], gsum[:]))
                link(V.tensor_scalar(gsel[:, :, 0:1], gsel[:, :, 1:2], -1.0, 1.0, ALU.mult, ALU.add))
                mark(V.tensor_tensor(gtop[:], gtop[:], gsum[:], ALU.mult))
                link(V.tensor_tensor(gsel[:], gsel[:], esum[:], ALU.mult))
                link(V.tensor_tensor(gsel[:], gsel[:], gtop[:].to_broadcast([P, TT, NGRP]), ALU.mult))
                for d in range(1, EPG):
                    link(V.tensor_tensor(cmp[:, :, :, 0:EPG - d], ee[:, :, :, d:EPG], ee[:, :, :, 0:EPG - d], ALU.is_gt))
                    link(V.tensor_tensor(rank[:, :, :, 0:EPG - d], rank[:, :, :, 0:EPG - d], cmp[:, :, :, 0:EPG - d], ALU.add))
                    link(V.tensor_tensor(rank[:, :, :, d:EPG], rank[:, :, :, d:EPG], cmp[:, :, :, 0:EPG - d], ALU.subtract))
                link(V.tensor_scalar(rank[:], rank[:], 1.5, None, ALU.is_lt))
                link(V.tensor_tensor(rank[:], rank[:], ee, ALU.mult))
                link(V.tensor_tensor(we[:], rank[:], gsel[:].unsqueeze(3).to_broadcast([P, TT, NGRP, EPG]), ALU.mult))

            def stage_f(i, a):
                base = BASE[("f", a)]
                T = Tiles(i, base)
                y = src[a]
                dve.wait_ge(s_spl, i * 2 * NI + 2 * NI)
                for c in range(CT):
                    free(V.tensor_copy(nT[:, c, :], T.next()))
                for h in range(TT // 2):
                    yy = y[:, 2 * h:2 * h + 2, :]
                    free(V.tensor_tensor(yy, yy, T.next().rearrange("p (t n) -> p t n", t=2), ALU.add))
                dve.wait_ge(s_mf, i * N_MISC + base + T.j)
                mean_square_rsqrt(y)
                for tt in range(TT):
                    mark(V.scalar_tensor_tensor(out=y[:, tt, :], in0=y[:, tt, :], scalar=ny[:, tt:tt + 1], in1=n1_bc[:],
                                                op0=ALU.mult, op1=ALU.mult))
                ready(s_xr)
                for c in range(CT):
                    free(V.tensor_copy(cT[:, c, :], T.next()))
                route(i, a, T.next()[:, 0:TT * 16].rearrange("p (t n) -> p t n", t=TT)[:, :, 0:NR])
                for net in range(2):
                    for j in range(HT):
                        nth = net * HT + j
                        dve.wait_ge(s_th, i * 4 * HT + a * 2 * HT + nth + 1)
                        if nth >= 2:
                            dve.wait_ge(s_mf, i * N_MISC + base + T.j)
                        free(V.scalar_tensor_tensor(out=uu[:, nth % 2, :], in0=th[:, nth % 2, :], scalar=1.0, in1=T.next(),
                                                    op0=ALU.add, op1=ALU.mult))
                        dve.wait_ge(s_mf, i * N_MISC + base + T.j)
                        free(V.scalar_tensor_tensor(out=hT[:, j, :], in0=uu[:, nth % 2, :], scalar=0.5, in1=T.next(),
                                                    op0=ALU.mult, op1=ALU.mult))
                    if net == 0:
                        for h in range(TT // 2):
                            yy = y[:, 2 * h:2 * h + 2, :]
                            free(V.tensor_tensor(yy, yy, T.next().rearrange("p (t n) -> p t n", t=2), ALU.add))
                for tt in range(TT):
                    for e in range(0, NE, 2):
                        r = T.next()
                        dve.wait_ge(s_mf, i * N_MISC + base + T.j - 1)
                        link(V.scalar_tensor_tensor(out=y[:, tt, :], in0=r[:, 0:D], scalar=we[:, tt, e // EPG, e % EPG:e % EPG + 1],
                                                    in1=y[:, tt, :], op0=ALU.mult, op1=ALU.add))
                        e += 1
                        free(V.scalar_tensor_tensor(out=y[:, tt, :], in0=r[:, D:2 * D], scalar=we[:, tt, e // EPG, e % EPG:e % EPG + 1],
                                                    in1=y[:, tt, :], op0=ALU.mult, op1=ALU.add))
                assert T.j == F_TILES
                dve.wait_ge(s_mf, i * N_MISC + base + T.j)
                mean_square_rsqrt(y)
                for tt in range(TT):
                    mark(V.scalar_tensor_tensor(out=sa[a][:, tt, :], in0=y[:, tt, :], scalar=ny[:, tt:tt + 1], in1=n2_bc[:],
                                                op0=ALU.mult, op1=ALU.mult))
                until(k[0])
                mark(V.tensor_tensor(sa[a][:], sa[a][:], xin[a][:], ALU.add))
                ready(s_fin)

            stage = {"p1": stage_p1, "p2": stage_p2, "f": stage_f}

            def row_max(i, l, p):
                q = l * PAIRS + p
                gi = q // (PAIRS // NG)
                h, t2 = p % (PAIRS // NG) // 2, p % 2
                dve.wait_ge(s_sS, i * NI * PAIRS + q + 1)
                V.tensor_reduce(negm[:, gi % 2, 2 * t2:2 * t2 + 2, h], ps[:, 2 + 2 * (q % 2):4 + 2 * (q % 2), :], AX.X, ALU.max,
                                negate=True).then_inc(s_sF, 1)
                if (p + 1) % (PAIRS // NG) == 0:
                    dve.wait_ge(s_sF, i * NI * PAIRS + q + 1)
                    m, r, o = negm[:, gi % 2], mres[:, gi % 2], m3[:, gi % 2]
                    link(V.tensor_copy(o[:, :, 0, :], m))
                    link(V.tensor_tensor(r, m, o[:, :, 0, :], ALU.subtract))
                    link(V.tensor_copy(o[:, :, 1, :], r))
                    mark(V.tensor_tensor(o[:, :, 2, :], r, o[:, :, 1, :], ALU.subtract))
                    ready(s_m3)

            def max_turned(i, gi):
                c = turns.take()
                dve.wait_ge(s_x7, i * N_X7 + c + 1)
                if gi >= 2:
                    dve.wait_ge(s_mrow, i * NI * NG * 48 + 48 * (gi - 1))
                mark(V.tensor_copy(mTs[:, gi % 2, :], ps[:, 7, 0:L // 2].bitcast(BF16)[0:NPART * HG, :]))
                until(k[0])
                dve.sem_inc(s_x7f, 1)
                dve.sem_inc(s_mts, 1)

            def heads_out(i, gi):
                l, g = divmod(gi, NG)
                a = l % 2
                c = turns.take()
                dve.wait_ge(s_x7, i * N_X7 + c + 1)
                o = ps[:, 7, :].rearrange("p (t h d) -> p t h d", t=TT, h=HG)
                link(V.reciprocal(rec[:], o[:, :, :, DH]))
                mark(V.tensor_tensor(sa[a][:, :, g * HG * DH:(g + 1) * HG * DH].rearrange("p t (h d) -> p t h d", h=HG),
                                     o[:, :, :, 0:DH], rec[:].unsqueeze(3).to_broadcast([P, TT, HG, DH]), ALU.mult))
                until(k[0])
                dve.sem_inc(s_x7f, 1)
                if g == NG - 1:
                    if l < 2:
                        link(V.scalar_tensor_tensor(out=xin[a][:], in0=sa[a][:], scalar=tg[:, 0:1], in1=xin[a][:],
                                                    op0=ALU.mult, op1=ALU.add))
                        layernorm(xin[a], src[a])
                        dve.sem_inc(s_src, 1)
                    else:
                        dve.sem_inc(s_sa, 1)

            with dve.Fori(0, B // 2) as i:
                it[0] = i * LINKS + SETUP
                k[0] = 0
                turns = Turns()
                dve.wait_ge(s_st, i * 32)
                dve.wait_ge(s_mrow, i * NI * NG * 48)
                for a in range(2):
                    dve.wait_ge(s_ldx[a], i * 16 + 16)
                    layernorm(xin[a], src[a])
                    dve.sem_inc(s_src, 1)
                    if a == 0:
                        stage_p1(i, 0)
                for p in range(LEAD):
                    row_max(i, 0, p)
                max_turned(i, 0)
                for l in range(NI):
                    for g in range(NG):
                        gi = l * NG + g
                        for s in range(STEPS):
                            if s % 2:
                                p = (g * STEPS + s) // 2 + LEAD
                                if p < PAIRS:
                                    row_max(i, l, p)
                                elif l + 1 < NI:
                                    row_max(i, l + 1, p - PAIRS)
                            if s == 8 and gi > 0:
                                heads_out(i, gi - 1)
                            if s == 10 and gi + 1 < NI * NG:
                                max_turned(i, gi + 1)
                            for kind, a in stages_at(l, g, s):
                                stage[kind](i, a)
                heads_out(i, NI * NG - 1)
                stage_f(i, 1)
                assert k[0] == LINKS, k[0]

        @block.tensor
        def _(pe):
            MM, TR = nc.tensor.matmul, nc.tensor.transpose
            pe.wait_ge(s_id, 4)
            pe.wait_ge(s_wn, 48)
            for j, w in enumerate((src[0], src[1], sa[0])):
                for c in range(CT):
                    for o in range(CT):
                        last = TR(ps[:, j, c * D + o * P:c * D + (o + 1) * P], w[:, o, c * P:(c + 1) * P], identf[:])
                last.then_inc(s_wt, 1)
            pe.wait_ge(s_set, 2)
            pe.wait_ge(s_w, 16 * N_W)

            class Tiles:

                def __init__(self, i, base, used7, units):
                    self.i, self.base, self.j = i, base, 0
                    pe.wait_ge(s_x7f, i * N_X7 + used7)
                    pe.wait_ge(s_exp, i * NI * UNITS + units)

                def next(self):
                    if self.j >= 3:
                        self.evacuated(self.j - 2)
                    self.j += 1
                    return ps[:, MISC_BANKS[(self.j - 1) % 3], :]

                def evacuated(self, n):
                    pe.wait_ge(s_mf, self.i * N_MISC + self.base + n)

            def turn(T, t):
                for c in range(CT):
                    o = T.next()
                    for tt in range(TT):
                        last = TR(o[:, tt * P:(tt + 1) * P], t[:, tt, c * P:(c + 1) * P], identf[:])
                    last.then_inc(s_mt, 1)

            def product(o, terms):
                for n, (w, r) in enumerate(terms):
                    last = MM(o, w, r, start=(n == 0), stop=(n == len(terms) - 1))
                return last

            def stage_p1(i, a, T):
                pe.wait_ge(s_src, i * NI + a + 1)
                turn(T, src[a])
                pe.wait_ge(s_ldc, i * 32 + 16 * (a + 1))
                turn(T, ctxs)
                for X, r in ((0, nT), (1, cT)):
                    for o in range(CT):
                        b_ = T.next()
                        T.evacuated(2 + 2 * X)
                        product(b_, [(wT[:, X, k, o * P:(o + 1) * P], r[:, k, :]) for k in range(CT)]).then_inc(s_mt, 1)
                for h in range(TT // 2):
                    o = T.next()
                    for t in range(2):
                        tt = 2 * h + t
                        last = product(o[:, t * D:(t + 1) * D], [(cT[:, k, tt * P:(tt + 1) * P], wT[:, 2, k, :]) for k in range(CT)])
                    last.then_inc(s_mt, 1)

            def stage_p2(i, a, T):
                pe.wait_ge(s_src, i * NI + 2 + a + 1)
                turn(T, src[a])

                def halves(w, r):
                    for f in range(2):
                        o = T.next()
                        if f == 0:
                            T.evacuated(T.j - 1)
                        product(o, [(w_[:, f * P:(f + 1) * P], r_)
                                    for w_, r_ in zip(w, r)]).then_inc(s_mt, 1)

                halves([fq[:, k, :] for k in range(CT)], [nT[:, k, :] for k in range(CT)])
                product(T.next(), [(fkvc[:, k, :], nT[:, k, :]) for k in range(CT)]).then_inc(s_mt, 1)
                halves([fkv[0:DC, :]], [cT[0:DC, 0, :]])
                for h in range(TT // 2):
                    o = T.next()
                    for t in range(2):
                        tt = 2 * h + t
                        last = MM(o[:, t * D:(t + 1) * D], cT[DC:2 * DC, 0, tt * P:(tt + 1) * P], fkv[DC:2 * DC, :],
                                  start=True, stop=True)
                    last.then_inc(s_mt, 1)

            def stage_f(i, a, T):
                pe.wait_ge(s_sa, i * 2 + a + 1)
                turn(T, sa[a])
                for h in range(TT // 2):
                    o = T.next()
                    T.evacuated(2)
                    for t in range(2):
                        tt = 2 * h + t
                        last = product(o[:, t * D:(t + 1) * D], [(nT[:, k, tt * P:(tt + 1) * P], fo[:, k, :]) for k in range(CT)])
                    last.then_inc(s_mt, 1)
                pe.wait_ge(s_xr, i * 2 + a + 1)
                turn(T, src[a])
                o = T.next()
                T.evacuated(6)
                for tt in range(TT):
                    last = product(o[:, tt * 16:tt * 16 + NR], [(cT[:, k, tt * P:(tt + 1) * P], fg[:, k, :]) for k in range(CT)])
                last.then_inc(s_mt, 1)
                for net in range(2):
                    for j in range(HT):
                        for half in range(2):
                            c = half * HID + j * P
                            product(T.next(), [(fin[:, net, k, c:c + P], cT[:, k, :]) for k in range(CT)]).then_inc(s_mt, 1)
                    hidden = T.j
                    if net == 0:
                        for h in range(TT // 2):
                            o = T.next()
                            T.evacuated(hidden)
                            for t in range(2):
                                tt = 2 * h + t
                                last = product(o[:, t * D:(t + 1) * D],
                                               [(hT[:, k, tt * P:(tt + 1) * P], fout[:, k, :]) for k in range(HT)])
                            last.then_inc(s_mt, 1)
                for tt in range(TT):
                    for e in range(0, NE, 2):
                        o = T.next()
                        T.evacuated(max(hidden, T.j - 3))
                        product(o, [(hT[:, k, tt * P:(tt + 1) * P], w2[:, k, e:e + 2, :].rearrange("p e n -> p (e n)"))
                                    for k in range(HT)]).then_inc(s_mt, 1)
                assert T.j == F_TILES

            stage = {"p1": stage_p1, "p2": stage_p2, "f": stage_f}

            def run(i, kind, a, units):
                base = BASE[(kind, a)]
                T = Tiles(i, base, turns.n, units)
                stage[kind](i, a, T)
                T.evacuated(T.j)

            def max_pair(i, l, p):
                q = l * PAIRS + p
                gi = q // (PAIRS // NG)
                g = gi % NG
                h, t2 = p % (PAIRS // NG) // 2, p % 2
                if p % (PAIRS // NG) == 0:
                    pe.wait_ge(s_stk[g], (i * NI + gi // NG + 1) * 192)
                pe.wait_ge(s_sF, i * NI * PAIRS + max(q - 1, 0))
                for t in range(2):
                    tt = 2 * t2 + t
                    last = MM(ps[:, 2 + 2 * (q % 2) + t, :], qs[0:STK, g, h, tt * P:(tt + 1) * P], ks[0:STK, g, h, :],
                              start=True, stop=True)
                last.then_inc(s_sS, 1)

            def turn_max(i, gi):
                pe.wait_ge(s_m3, i * NI * NG + gi + 1)
                pe.wait_ge(s_x7f, i * N_X7 + turns.take())
                o = ps[:, 7, 0:L // 2].bitcast(BF16)
                for tt in range(TT):
                    last = TR(o[0:NPART * HG, tt * P:(tt + 1) * P],
                              m3[:, gi % 2, tt].rearrange("p s h -> p (s h)"), identb[:])
                last.then_inc(s_x7, 1)

            def turn_heads(i, gi):
                pe.wait_ge(s_oc, i * NI * NG + gi + 1)
                pe.wait_ge(s_x7f, i * N_X7 + turns.take())
                for tt in range(TT):
                    last = TR(ps[:, 7, tt * P:(tt + 1) * P], oT[:, tt * P:(tt + 1) * P], identf[:])
                last.then_inc(s_x7, 1)

            def values(i, gi, kt):
                l, g = divmod(gi, NG)
                kk = gi * TT + kt
                if kt == 0:
                    pe.wait_ge(s_oc, i * NI * NG + gi)
                    if g == 0:
                        pe.wait_ge(s_vp, i * NI + l + 1)
                pe.wait_ge(s_exp, i * NI * UNITS + HG * (kk + 1))
                for h in range(HG):
                    last = MM(ps[32 * h:32 * h + VM, 6, :], vp[l % 2][:, kt, g * HG + h, :], prob[:, kk % PROB_SLOTS, h, :],
                              start=(kt == 0), stop=(kt == TT - 1))
                last.then_inc(s_pv, 1)

            with pe.Fori(0, B // 2) as i:
                turns = Turns()
                run(i, "p1", 0, 0)
                for p in range(LEAD):
                    max_pair(i, 0, p)
                turn_max(i, 0)
                for l in range(NI):
                    for g in range(NG):
                        gi = l * NG + g
                        for s in range(STEPS):
                            u = gi * STEPS + s
                            kt, h = divmod(s, HG)
                            if s == 0:
                                pe.wait_ge(s_mrow, (i * NI * NG + gi + 1) * 48)
                            if u >= 2:
                                pe.wait_ge(s_exp, i * NI * UNITS + u - 1)
                            MM(ps[:, u % 2, :], ks[:, g, h, kt * P:(kt + 1) * P], qs[:, g, h, :],
                               start=True, stop=True).then_inc(s_sT, 1)
                            if s % 2:
                                p = (g * STEPS + s) // 2 + LEAD
                                if p < PAIRS:
                                    max_pair(i, l, p)
                                elif l + 1 < NI:
                                    max_pair(i, l + 1, p - PAIRS)
                            if s % HG == HG - 1 and (kt or gi):
                                values(i, *((gi, kt - 1) if kt else (gi - 1, TT - 1)))
                            if s == 8 and gi > 0:
                                turn_heads(i, gi - 1)
                            if s == 10 and gi + 1 < NI * NG:
                                turn_max(i, gi + 1)
                            for kind, a in stages_at(l, g, s):
                                run(i, kind, a, u + 1)
                values(i, NI * NG - 1, TT - 1)
                turn_heads(i, NI * NG - 1)
                run(i, "f", 1, NI * UNITS)


N_W = 29
LINKS = 450
BASE = {("p1", 0): 0, ("p1", 1): 10, ("p2", 0): 20, ("p2", 1): 29, ("f", 0): 38, ("f", 1): 38 + 41}


def turned_before_o(gi):
    return 0 if gi == 0 else 2 * gi + 1


def rope_table(L, dh, nh):
    inv = (np.float32(1.0) / np.float32(10000.0) ** (np.arange(0, dh, 2, dtype=np.float32) / np.float32(dh))).astype(np.float32)
    ang = np.arange(L, dtype=np.float32)[:, None] * inv[None, :]
    t = np.stack([np.cos(ang), np.sin(ang)]).astype(np.float32)
    return np.ascontiguousarray(np.repeat(t.transpose(0, 2, 1), nh, axis=1))


_INS = ["x", "ctx_1024", "g_xattn", "g_ffn", "L0_xattn_wq", "L0_xattn_bq", "L0_xattn_wk", "L0_xattn_bk", "L0_xattn_wv",
        "L0_xattn_bv", "L0_ffn_Wq", "L0_ffn_Wk_c", "L0_ffn_Wv_c", "L0_ffn_Wk", "L0_ffn_Wv", "L0_ffn_Wo", "L0_ffn_W_shared_in",
        "L0_ffn_W_shared_out", "L0_ffn_W1_shared", "L0_ffn_W2_experts", "L0_ffn_Wg_gate", "L0_ffn_We_gate",
        "L0_ffn_group_bias", "L0_ffn_expert_bias", "L0_ffn_norm1_w", "L0_ffn_norm2_w"]


def kernel(**inputs):
    import concourse.bacc as _bacc
    from concourse.bass_utils import run_bass_kernel_spmd as _run

    nc = _bacc.Bacc("TRN2", target_bir_lowering=False, num_devices=1)
    arrays, args = {}, []
    given = {name: np.ascontiguousarray(inputs[name]) for name in _INS}
    B, L, D = given["x"].shape
    given["rope"] = rope_table(L, 16, 16)
    for name, a in given.items():
        arrays[f"in_{name}_dram"] = a
        args.append(nc.dram_tensor(f"in_{name}_dram", a.shape, mybir.dt.from_np(a.dtype), kind="ExternalInput").ap())
    args.append(nc.dram_tensor("out_dram", (B, L, D), F32, kind="ExternalOutput").ap())
    flamingo_block(nc, *args)
    r = _run(nc, [arrays], core_ids=[0])
    return r.results[0]["out_dram"]
```

```python
from contextlib import ExitStack

import numpy as np
import concourse.bass as bass
from concourse import mybir

F32 = mybir.dt.float32
BF16 = mybir.dt.bfloat16
I32 = mybir.dt.int32
ALU = mybir.AluOpType
ACT = mybir.ActivationFunctionType
AX = mybir.AxisListType

P = 128
HG = 4
NTERM = 6
NPART = 3
MPART = 2
Q_PART = [0, 0, 0, 1, 1, 2]
K_PART = [0, 1, 2, 0, 1, 0]
LEAD = 12
PROB_SLOTS = 3
AT_COPY, AT_HEADS, AT_MAX, AT_ROWS = 4, 8, 9, 11
SCORE_BANKS = [0, 1, 7]
MISC_BANKS = SCORE_BANKS


def flamingo_block(nc, x, ctx_in, g_xattn, g_ffn, wq, bq, wk, bk, wv, bv,
                   f_wq, f_wkc, f_wvc, f_wk, f_wv, f_wo, f_in, f_out, f_w1, f_w2,
                   f_gg, f_ge, f_gb, f_eb, n1, n2, rope, out):
    B, L, D = x.shape
    NH = 16
    DH = D // NH
    TT = L // P
    CT = D // P
    NG = NH // HG
    HID = f_out.shape[0]
    HT = HID // P
    NE = f_w2.shape[0]
    NGRP = f_gg.shape[1]
    EPG = NE // NGRP
    NR = NGRP + NE
    DC = f_wkc.shape[1]
    STK = NTERM * DH
    KROWS = STK + MPART
    NI = 4
    PAIRS = NH * TT // 2
    UNITS = NH * TT
    KTS = NG * TT
    STEPS = UNITS // NG
    SC = 1.0 / float(DH) ** 0.5
    assert (L, D, DH, CT, TT, DC, EPG) == (512, 256, 16, 2, 4, 64, 4)

    P1_TILES, P2_TILES, FA_TILES, FB_TILES = 10, 9, 4, 3 + 2 * 2 * HT + 2 + TT * NE // 2
    START = [("n1", 0), ("p1", 0), ("n1", 1), ("p1", 1)]
    HOOKS = {(1, 0, 11): [("s2", 0)], (1, 1, 0): [("n2", 0)], (1, 1, 3): [("p2", 0)],
             (2, 0, 11): [("s2", 1)], (2, 1, 0): [("n2", 1)], (2, 1, 3): [("p2", 1)],
             (3, 0, 13): [("fa", 0)], (3, 1, 3): [("nf", 0)], (3, 1, 7): [("fb", 0)]}
    END = [("fa", 1), ("nf", 1), ("fb", 1)]
    BASE, N_MISC = {}, 0
    for stages in [START, *(HOOKS[k_] for k_ in sorted(HOOKS)), END]:
        for kind, a_ in stages:
            BASE[kind, a_] = N_MISC
            N_MISC += {"p1": P1_TILES, "p2": P2_TILES, "fa": FA_TILES, "fb": FB_TILES}.get(kind, 0)
    N_TURN = 2 * NI * NG
    N_RING = NI * PAIRS + N_TURN
    NORMS = [("x", 0), ("x", 1), ("x1", 0), ("x1", 1), ("y", 0), ("out", 0), ("y", 1), ("out", 1)]
    NN = len(NORMS)
    VM = DH + 1

    es = ExitStack()
    with es:
        def sb(name, shape, dt):
            return es.enter_context(nc.sbuf_tensor(name, shape, dt))

        def sem(name):
            return es.enter_context(nc.semaphore(name))

        wT = sb("wT", [P, 3, CT, D], F32)
        fq = sb("fq", [P, CT, D], F32)
        fkvc = sb("fkvc", [P, CT, 2 * DC], F32)
        fkv = sb("fkv", [P, D], F32)
        fo = sb("fo", [P, CT, D], F32)
        fin = sb("fin", [P, 2, CT, 2 * HID], F32)
        fout = sb("fout", [P, HT, D], F32)
        w2 = sb("w2", [P, HT, NE, D], F32)
        fg = sb("fg", [P, CT, NR], F32)
        bqk = sb("bqk", [P, 2, CT], F32)
        bv_bc = sb("bv_bc", [P, D], F32)
        n1_bc = sb("n1_bc", [P, D], F32)
        n2_bc = sb("n2_bc", [P, D], F32)
        gb_bc = sb("gb_bc", [P, NR], F32)
        gates = sb("gates", [P, 2], F32)
        tg = sb("tg", [P, 2], F32)
        rope_sb = sb("rope_sb", [P, 2, L], F32)
        identf = sb("identf", [P, P], F32)
        identb = sb("identb", [P, P], BF16)
        rank0 = sb("rank0", [P, TT, NGRP, EPG], F32)
        xin = [sb(f"xin{i}", [P, TT, D], F32) for i in range(2)]
        ctxs = sb("ctxs", [P, TT, D], F32)
        src = [sb(f"src{i}", [P, TT, D], F32) for i in range(2)]
        sa = [sb(f"sa{i}", [P, TT, D], F32) for i in range(2)]
        nT = sb("nT", [P, CT, L], F32)
        cT = sb("cT", [P, CT, L], F32)
        qk = [sb(f"qk{i}", [P, 2, L], F32) for i in range(2)]
        hT = sb("hT", [P, HT, L], F32)
        rb = [hT[:, 2 * X:2 * X + 2, :] for X in range(2)]
        parts = [sb(f"parts{i}", [P, NPART, 2, L], BF16) for i in range(2)]
        qs = sb("qs", [KROWS, NG, HG, L], BF16)
        ks = sb("ks", [KROWS, NG, HG, L], BF16)
        vp = [sb(f"vp{i}", [P, TT, NH, VM], F32) for i in range(2)]
        prob = sb("prob", [P, PROB_SLOTS, HG, L], F32)
        oT = sb("oT", [P, L], F32)
        negm = sb("negm", [P, 2, TT, HG], F32)
        m2 = sb("m2", [P, 2, TT, MPART, HG], BF16)
        mTs = sb("mTs", [MPART * HG, 2, L], BF16)
        rec = sb("rec", [P, TT, HG], F32)
        bst = sb("bst", [P, TT, 6], F32)
        mean = sb("mean", [P, TT], F32)
        mdif = sb("mdif", [P, TT], F32)
        nvar = sb("nvar", [P, TT], F32)
        scale_ = sb("scale", [P, NN, TT], F32)
        shift_ = sb("shift", [P, NN, TT], F32)
        mhalf = sb("mhalf", [P, TT], F32)
        th = qk[0]
        uu = ctxs[:].rearrange("p (j t) c -> p j (t c)", j=2)
        lg = sb("lg", [P, TT, NR], F32)
        gmx = sb("gmx", [P, TT, 1], F32)
        emx = sb("emx", [P, TT, NGRP], F32)
        zr = sb("zr", [P, TT, NR], F32)
        ez = sb("ez", [P, TT, NR], F32)
        gsum = sb("gsum", [P, TT, 1], F32)
        gtop = sb("gtop", [P, TT, 1], F32)
        esum = sb("esum", [P, TT, NGRP], F32)
        gsel = sb("gsel", [P, TT, NGRP], F32)
        rank = sb("rank", [P, TT, NGRP, EPG], F32)
        cmp = sb("cmp", [P, TT, NGRP, EPG], F32)
        we = sb("we", [P, TT, NGRP, EPG], F32)

        ps = es.enter_context(nc.psum_tensor("ps", [P, 8, L], F32))
        scrq = nc.dram_tensor("scrq", [2, NH, NTERM, DH, L], BF16, kind="Internal").ap()
        scrk = nc.dram_tensor("scrk", [2, NH, NPART, DH, L], BF16, kind="Internal").ap()

        s_w = sem("large_weights_loaded")
        s_ws = sem("small_weights_loaded")
        s_wn = sem("xattn_weights_loaded")
        s_id = sem("identity_steps")
        s_wt = sem("weight_transposed")
        s_wtd = sem("weight_copied")
        s_set = sem("setup_done")
        s_tg = sem("gate_tanh")
        s_ldx = [sem(f"x_loaded{i}") for i in range(2)]
        s_ldc = sem("ctx_loaded")
        s_src = sem("normed_ready")
        s_mt = sem("misc_full")
        s_mf = sem("misc_free")
        s_k1 = sem("k_first_part_ready")
        s_spl = [sem(f"parts_ready{i}") for i in range(2)]
        s_bst = sem("row_statistics")
        s_ny = sem("row_scale_ready")
        s_hd = sem("heads_ready")
        s_x1 = sem("x1_ready")
        s_pool = sem("pool_chain")
        s_scr = [sem(f"scratch_written{i}") for i in range(2)]
        s_stk = [sem(f"stack_loaded{g}") for g in range(NG)]
        s_vp = sem("values_ready")
        s_rf = sem("ring_full")
        s_re = sem("ring_emptied")
        s_m2 = sem("maximum_parts")
        s_mts = sem("maximum_turned")
        s_mrow = sem("maximum_rows")
        s_sT = sem("score_full")
        s_exp = sem("exp_done")
        s_pv = sem("value_product")
        s_oc = sem("value_copied")
        s_sa = sem("self_attention_ready")
        s_th = sem("tanh_ready")
        s_xr = sem("block_normed")
        s_zr = sem("router_shifted")
        s_ez = sem("router_exp")
        s_fin = sem("result_ready")
        s_st = sem("result_stored")
        s_dve = sem("dve_chain")
        s_held = sem("waits_passed")


        LOOPED = [*s_ldx, s_ldc, s_src, s_mt, s_mf, s_k1, *s_spl, s_bst, s_ny, s_hd, s_x1, *s_scr, *s_stk, s_vp, s_rf, s_re, s_m2, s_mts, s_mrow,
                  s_sT, s_exp, s_pv, s_oc, s_sa, s_th, s_xr, s_zr, s_ez, s_fin, s_st, s_pool]

        block = es.enter_context(nc.Block())

        def turned_heads():
            n, after = LEAD + 1, []
            for gi in range(NI * NG):
                for s in range(STEPS):
                    n += s % 2 and (gi * STEPS + s) // 2 + LEAD < NI * PAIRS
                    if s == AT_HEADS and gi > 0:
                        n += 1
                        after.append(n)
                    n += s == AT_MAX and gi + 1 < NI * NG
            assert n + 1 == N_RING and N_RING % 2 == 0
            return after

        turned = turned_heads()

        class Ring:
            n = 0

            def take(self):
                self.n += 1
                return self.n - 1, 2 + 2 * ((self.n - 1) % 2)

        @block.sync
        def _(sp):
            for s_, d_ in ((src[0], wq), (src[1], wk), (sa[0], wv)):
                sp.dma_start(s_[:, 0:CT, :], d_.rearrange("(o p) c -> p o c", p=P)).then_inc(s_wn, 16)
            small = (
                (bqk[:, 0, :], bq.rearrange("(o p) -> p o", p=P)),
                (bqk[:, 1, :], bk.rearrange("(o p) -> p o", p=P)),
                (bv_bc[:], bv.unsqueeze(0).to_broadcast([P, D])),
                (gates[:, 0:1], g_xattn.unsqueeze(0).to_broadcast([P, 1])),
                (gates[:, 1:2], g_ffn.unsqueeze(0).to_broadcast([P, 1])),
                (n2_bc[:], n2.unsqueeze(0).to_broadcast([P, D])),
                (hT[:, 0, :].rearrange("p (k n) -> p k n", k=CT), f_wq.rearrange("(k p) n -> p k n", p=P)),
                (hT[0:DC, 1, 0:D], f_wk),
            )
            assert len(small) == N_SMALL
            for d_, s_ in small:
                sp.dma_start(d_, s_, allow_slow_non_contiguous=True).then_inc(s_ws, 16)
            sp.wait_ge(s_set, 4)

            def stack(i, l):
                par = l % 2
                for g in range(NG):
                    sp.wait_ge(s_stk[g], PRIMED + i * NI * 64 + max(l - 1, 0) * 64)
                    sp.sem_inc(s_held, 1)

                def put(scr, r, X, part):
                    for o in range(2):
                        if l < 2:
                            d_ = scr[par, o * NH // 2:(o + 1) * NH // 2, r]
                        else:
                            d_ = scr[par, :, r, o * DH // 2:(o + 1) * DH // 2].rearrange("h d t -> d h t")
                        sp.dma_start(d_, parts[X][:, part, o, :]).then_inc(s_scr[X], 16)

                sp.wait_ge(s_spl[0], PRIMED + i * NI + l + 1)
                sp.sem_inc(s_held, 1)
                for r in range(NTERM):
                    put(scrq, r, 0, Q_PART[r])
                sp.wait_ge(s_spl[1], PRIMED + i * NI + l + 1)
                sp.sem_inc(s_held, 1)
                for r in range(NPART):
                    put(scrk, r, 1, r)
                sp.wait_ge(s_scr[0], PRIMED + i * NI * 32 * NTERM + 32 * NTERM * (l + 1))
                sp.sem_inc(s_held, 1)
                sp.wait_ge(s_scr[1], PRIMED + i * NI * 32 * NPART + 32 * NPART * (l + 1))
                sp.sem_inc(s_held, 1)
                for g in range(NG):
                    if l == 0:
                        sp.wait_ge(s_sT, PRIMED + i * NI * UNITS)
                        sp.sem_inc(s_held, 1)
                    else:
                        sp.wait_ge(s_sT, PRIMED + i * NI * UNITS + (l - 1) * UNITS + (g + 1) * STEPS)
                        sp.sem_inc(s_held, 1)
                    h_ = slice(g * HG, (g + 1) * HG)
                    sp.dma_start(qs[0:STK, g], scrq[par, h_].rearrange("h r d t -> (r d) h t")).then_inc(s_stk[g], 16)
                    row = 0
                    for n in range(NPART, 0, -1):
                        sp.dma_start(ks[row:row + n * DH, g], scrk[par, h_, 0:n].rearrange("h r d t -> (r d) h t")).then_inc(s_stk[g], 16)
                        row += n * DH

            with sp.Fori(0, B // 2) as i:
                for a in range(2):
                    sp.wait_ge(s_fin, PRIMED + i * 2)
                    sp.sem_inc(s_held, 1)
                    sp.dma_start(xin[a][:], x[bass.ds(i * 2 + a, 1)].rearrange("b (t p) c -> p (b t) c", p=P)).then_inc(s_ldx[a], 16)
                    sp.wait_ge(s_mf, PRIMED + i * N_MISC + 4 * a)
                    sp.sem_inc(s_held, 1)
                    sp.dma_start(ctxs[:], ctx_in[bass.ds(i * 2 + a, 1)].rearrange("b (t p) c -> p (b t) c", p=P)).then_inc(s_ldc, 16)
                for l in range(NI):
                    stack(i, l)
                for a in range(2):
                    sp.wait_ge(s_fin, PRIMED + i * 2 + a + 1)
                    sp.sem_inc(s_held, 1)
                    sp.dma_start(out[bass.ds(i * 2 + a, 1)].rearrange("b (t p) c -> p (b t) c", p=P), sa[a][:]).then_inc(s_st, 16)
            sp.wait_ge(s_st, PRIMED + 16 * B)

        @block.gpsimd
        def _(pool):
            k = [0]

            it = [0]

            def link(ins):
                k[0] += 1
                ins.then_inc(s_pool, 1)
                pool.wait_ge(s_pool, PRIMED + it[0] + k[0])
                pool.sem_inc(s_held, 1)

            for s_ in LOOPED:
                pool.sem_inc(s_, PRIMED)
            pool.sem_inc(s_set, 1)
            pool.memset(identf[:], 0.0).then_inc(s_id, 1)
            pool.memset(identb[:], 0.0).then_inc(s_id, 1)
            pool.wait_ge(s_id, 2)
            for m in (identf, identb):
                pool.affine_select(out=m[:], in_=m[:], compare_op=ALU.not_equal, fill=1.0, base=0,
                                   pattern=[[-1, P]], channel_multiplier=1).then_inc(s_id, 1)

            pool.memset(mhalf[:], -0.5).then_inc(s_set, 1)

            def row_scale(i, kind, a):
                e = NORMS.index((kind, a))
                layer = kind in ("x", "x1")
                pool.wait_ge(s_bst, PRIMED + i * NN + e + 1)
                pool.tensor_tensor(mdif[:], bst[:, :, 1], bst[:, :, 4], ALU.subtract)
                pool.tensor_tensor(mean[:], bst[:, :, 1], bst[:, :, 4], ALU.add)
                link(pool.tensor_tensor(nvar[:], bst[:, :, 2], bst[:, :, 5], ALU.add))
                pool.tensor_tensor(mdif[:], mdif[:], mdif[:], ALU.mult)
                pool.tensor_scalar(mean[:], mean[:], -0.5, None, ALU.mult)
                link(pool.tensor_scalar(nvar[:], nvar[:], 1.0 / D, 1e-5 if layer else 1e-6, ALU.mult, ALU.add))
                link(pool.tensor_scalar(mdif[:], mdif[:], 0.25, None, ALU.mult))
                link(pool.tensor_tensor(nvar[:], nvar[:], mdif[:], ALU.add))
                if not layer:
                    link(pool.tensor_tensor(mdif[:], mean[:], mean[:], ALU.mult))
                    link(pool.tensor_tensor(nvar[:], nvar[:], mdif[:], ALU.add))
                link(pool.tensor_tensor(scale_[:, e], nvar[:], mhalf[:], ALU.pow))
                if layer:
                    link(pool.tensor_tensor(shift_[:, e], mean[:], scale_[:, e], ALU.mult))
                pool.sem_inc(s_ny, 1)

            def last_parts(i, l):
                pool.wait_ge(s_k1, PRIMED + i * NI + l + 1)
                pool.sem_inc(s_held, 1)
                link(pool.tensor_scalar(parts[1][:, 1], qk[1][:], 1.0, None, ALU.mult))
                link(pool.tensor_tensor(parts[1][:, 2], qk[1][:], parts[1][:, 1], ALU.subtract))
                pool.sem_inc(s_spl[1], 1)

            def add_heads(i, gi):
                g = gi % NG
                xs = xin[gi // NG][:, :, g * HG * DH:(g + 1) * HG * DH]
                pool.wait_ge(s_hd, PRIMED + i * 2 * NG + gi + 1)
                link(pool.tensor_tensor(xs, xs, sa[gi // NG][:, :, g * HG * DH:(g + 1) * HG * DH], ALU.add))
                if g == NG - 1:
                    pool.sem_inc(s_x1, 1)

            stage = {"n1": lambda i, a: row_scale(i, "x", a), "p1": lambda i, a: last_parts(i, a),
                     "n2": lambda i, a: row_scale(i, "x1", a), "p2": lambda i, a: last_parts(i, 2 + a),
                     "nf": lambda i, a: row_scale(i, "y", a), "fb": lambda i, a: row_scale(i, "out", a)}
            with pool.Fori(0, B // 2) as i:
                k[0], it[0] = 0, i * POOL_LINKS
                for kind, a in START:
                    stage[kind](i, a)
                for l in range(NI):
                    for g in range(NG):
                        gi = l * NG + g
                        for s in range(STEPS):
                            if s == AT_HEADS and 0 < gi <= 2 * NG:
                                add_heads(i, gi - 1)
                            for kind, a in HOOKS.get((l, g, s), []):
                                if kind in stage:
                                    stage[kind](i, a)
                for kind, a in END:
                    if kind in stage:
                        stage[kind](i, a)
                assert k[0] == POOL_LINKS, k[0]

        @block.scalar
        def _(act):
            act.wait_ge(s_ws, 16 * N_SMALL)
            nc.scalar.activation(tg[:], gates[:], ACT.Tanh).then_inc(s_tg, 1)
            act.wait_ge(s_ldx[1], 1 + 16)
            large = [
                (rope_sb[:], rope.rearrange("s p t -> p s t")),
                (fkvc[:, :, 0:DC], f_wkc.rearrange("(k p) n -> p k n", p=P)),
                (fkvc[:, :, DC:2 * DC], f_wvc.rearrange("(k p) n -> p k n", p=P)),
                (fkv[DC:2 * DC, :], f_wv),
                (fo[:], f_wo.rearrange("(k p) n -> p k n", p=P)),
                (n1_bc[:], n1.unsqueeze(0).to_broadcast([P, D])),
                (gb_bc[:, 0:NGRP], f_gb.unsqueeze(0).to_broadcast([P, NGRP])),
                (gb_bc[:, NGRP:NR], f_eb.unsqueeze(0).to_broadcast([P, NE])),
                (fg[:, :, 0:NGRP], f_gg.rearrange("(k p) n -> p k n", p=P)),
                (fg[:, :, NGRP:NR], f_ge.rearrange("(k p) n -> p k n", p=P)),
                (fin[:, 0], f_in.rearrange("(k p) n -> p k n", p=P)),
                (fin[:, 1], f_w1.rearrange("(k p) n -> p k n", p=P)),
                (fout[:], f_out.rearrange("(k p) n -> p k n", p=P)),
            ] + [(w2[:, :, e, :], f_w2[e].rearrange("(k p) n -> p k n", p=P)) for e in range(NE)]
            assert len(large) == N_LARGE
            for d_, s_ in large:
                act.dma_start(d_, s_).then_inc(s_w, 16)

            def copy_values(i, gi):
                act.wait_ge(s_pv, PRIMED + i * NI * KTS + TT * (gi + 1))
                if gi:
                    act.wait_ge(s_rf, PRIMED + i * N_RING + turned[gi - 1])
                nc.scalar.activation(oT[:], ps[:, 6, :], ACT.Copy).then_inc(s_oc, 1)

            def max_rows(i, gi):
                act.wait_ge(s_mts, PRIMED + i * NI * NG + gi + 1)
                for t in range(MPART):
                    act.dma_start(qs[STK + t:STK + t + 1, gi % NG, :, :],
                                  mTs[t * HG:(t + 1) * HG, gi % 2, :]).then_inc(s_mrow, 16)

            def normalise(i, kind, a):
                e = NORMS.index((kind, a))
                act.wait_ge(s_ny, PRIMED + i * NN + e + 1)
                for tt in range(TT):
                    last = nc.scalar.activation(src[a][:, tt, :], xin[a][:, tt, :], ACT.Identity,
                                                bias=shift_[:, e, tt:tt + 1], scale=scale_[:, e, tt:tt + 1])
                last.then_inc(s_src, 1)

            def ffn(i, a):
                base = BASE["fb", a]
                act.wait_ge(s_spl[0], PRIMED + i * NI + NI)
                act.wait_ge(s_zr, PRIMED + i * 2 + a + 1)
                nc.scalar.activation(ez[:], zr[:], ACT.Exp).then_inc(s_ez, 1)
                for net in range(2):
                    for j in range(HT):
                        t = base + 3 + net * (2 * HT + 2) + 2 * j
                        act.wait_ge(s_mt, PRIMED + i * N_MISC + t + 1)
                        nth = net * HT + j
                        if nth >= 2:
                            tp = t - 4 if j >= 2 else t - 6
                            act.wait_ge(s_mf, PRIMED + i * N_MISC + tp + 1)
                        nc.scalar.activation(th[:, nth % 2, :], ps[:, MISC_BANKS[(t - base) % 3], :],
                                             ACT.Tanh, scale=0.5).then_inc(s_th, 1)

            with act.Fori(0, B // 2) as i:
                act.wait_ge(s_pv, PRIMED + i * NI * KTS)
                act.wait_ge(s_mf, PRIMED + i * N_MISC)
                act.wait_ge(s_fin, PRIMED + i * 2)
                for kind, a in START:
                    if kind == "n1":
                        normalise(i, "x", a)
                max_rows(i, 0)
                for l in range(NI):
                    for g in range(NG):
                        gi = l * NG + g
                        for s in range(STEPS):
                            u = gi * STEPS + s
                            kt = gi * TT + s // HG
                            act.wait_ge(s_sT, PRIMED + i * NI * UNITS + u + 1)
                            if s % HG == 0 and kt >= PROB_SLOTS:
                                act.wait_ge(s_pv, PRIMED + i * NI * KTS + kt - PROB_SLOTS + 1)
                            nc.scalar.activation(prob[:, kt % PROB_SLOTS, s % HG, :], ps[:, SCORE_BANKS[u % 3], :],
                                                 ACT.Exp, scale=SC).then_inc(s_exp, 1)
                            if s == AT_COPY and gi > 0:
                                copy_values(i, gi - 1)
                            if s == AT_ROWS and gi + 1 < NI * NG:
                                max_rows(i, gi + 1)
                            for kind, a in HOOKS.get((l, g, s), []):
                                if kind == "n2":
                                    normalise(i, "x1", a)
                                if kind == "fb":
                                    ffn(i, a)
                copy_values(i, NI * NG - 1)
                ffn(i, 1)

        @block.vector
        def _(dve):
            k = [0]
            it = [0]

            def link(ins):
                k[0] += 1
                ins.then_inc(s_dve, 1)
                dve.wait_ge(s_dve, it[0] + k[0])

            def mark(ins):
                k[0] += 1
                ins.then_inc(s_dve, 1)
                return k[0]

            def until(n):
                dve.wait_ge(s_dve, it[0] + n)

            V = nc.vector
            V.memset(ps[:, 6, :], 0.0).then_inc(s_set, 1)
            V.memset(ks[STK:KROWS], 1.0).then_inc(s_dve, 1)
            V.memset(vp[0][:, :, :, DH:VM], 1.0).then_inc(s_dve, 1)
            V.memset(vp[1][:, :, :, DH:VM], 1.0).then_inc(s_dve, 1)
            for e in range(EPG):
                V.memset(rank0[:, :, :, e:e + 1], float(e)).then_inc(s_dve, 1)
            for j in range(3):
                dve.wait_ge(s_wt, j + 1)
                V.tensor_copy(wT[:, j], ps[:, j, :].rearrange("p (c n) -> p c n", c=CT)).then_inc(s_wtd, 1)
            dve.wait_ge(s_wtd, 3)
            dve.wait_ge(s_ws, 16 * N_SMALL)
            dve.wait_ge(s_tg, 1)
            V.tensor_scalar(n2_bc[:], n2_bc[:], tg[:, 1:2], None, ALU.mult).then_inc(s_dve, 1)
            for w_, raw in [(fq[:, c_, :], hT[:, 0, c_ * D:(c_ + 1) * D]) for c_ in range(CT)] + [(fkv[0:DC, :], hT[0:DC, 1, 0:D])]:
                for f in range(2):
                    V.tensor_copy(w_[:, f * P:(f + 1) * P].rearrange("p (j h) -> p j h", h=NH),
                                  raw.rearrange("p (h j f) -> p f j h", f=2, j=DH // 2)[:, f]).then_inc(s_dve, 1)
            SETUP = 14
            dve.wait_ge(s_dve, SETUP)
            dve.sem_inc(s_set, 1)

            def statistics(i, kind, a, t):
                e = NORMS.index((kind, a))
                dve.wait_ge(s_ny, PRIMED + i * NN + e)
                for tt in range(TT):
                    mark(V.bn_stats(bst[:, tt, :], t[:, tt, :]))
                until(k[0])
                dve.sem_inc(s_bst, 1)

            def scaled(i, kind, a, dst, t, w):
                e = NORMS.index((kind, a))
                dve.wait_ge(s_ny, PRIMED + i * NN + e + 1)
                for tt in range(TT):
                    mark(V.scalar_tensor_tensor(out=dst[:, tt, :], in0=t[:, tt, :], scalar=scale_[:, e, tt:tt + 1], in1=w[:],
                                                op0=ALU.mult, op1=ALU.mult))
                until(k[0])

            def split(i, l, X):
                n = 32 * (NPART if X else NTERM)
                dve.wait_ge(s_scr[X], PRIMED + i * NI * n + l * n)
                link(V.tensor_copy(parts[X][:, 0], qk[X][:]))
                if X == 0:
                    link(V.tensor_tensor(qk[X][:], qk[X][:], parts[X][:, 0], ALU.subtract))
                    link(V.tensor_copy(parts[X][:, 1], qk[X][:]))
                    mark(V.tensor_tensor(parts[X][:, 2], qk[X][:], parts[X][:, 1], ALU.subtract))
                    until(k[0])
                    dve.sem_inc(s_spl[0], 1)
                else:
                    link(V.tensor_tensor(qk[X][:], qk[X][:], parts[X][:, 0], ALU.subtract))
                    dve.sem_inc(s_k1, 1)

            def ready(s):
                until(k[0])
                dve.sem_inc(s, 1)

            class Tiles:
                def __init__(self, i, base):
                    self.i, self.base, self.j = i, base, 0

                def next(self):
                    dve.wait_ge(s_mt, PRIMED + self.i * N_MISC + self.base + self.j + 1)
                    self.j += 1
                    return ps[:, MISC_BANKS[(self.j - 1) % 3], :]

            def stage_p1(i, a):
                base = BASE[("p1", a)]
                T = Tiles(i, base)
                for dst in (nT, cT):
                    for c in range(CT):
                        V.tensor_copy(dst[:, c, :], T.next()).then_inc(s_mf, 1)
                for X in range(2):
                    if X:
                        dve.wait_ge(s_spl[1], PRIMED + i * NI + a)
                    for o in range(CT):
                        V.tensor_scalar(qk[X][:, o, :], T.next(), bqk[:, X, o:o + 1], None, ALU.add).then_inc(s_mf, 1)
                    dve.wait_ge(s_mf, PRIMED + i * N_MISC + base + T.j)
                    split(i, a, X)
                dve.wait_ge(s_pv, PRIMED + i * NI * KTS)
                for h in range(TT // 2):
                    v = T.next().rearrange("p (t h d) -> p t h d", t=2, h=NH)
                    for t in range(2):
                        ins = V.tensor_tensor(vp[a][:, 2 * h + t, :, 0:DH], v[:, t],
                                              bv_bc[:].rearrange("p (h d) -> p h d", h=NH), ALU.add)
                        ins.then_inc(s_mf if t else s_dve, 1)
                    k[0] += 1
                dve.wait_ge(s_mf, PRIMED + i * N_MISC + base + T.j)
                until(k[0])
                dve.sem_inc(s_vp, 1)

            def stage_p2(i, a):
                base = BASE[("p2", a)]
                T = Tiles(i, base)
                l = 2 + a
                dve.wait_ge(s_w, 16 * N_LARGE)
                for c in range(CT):
                    V.tensor_copy(nT[:, c, :], T.next()).then_inc(s_mf, 1)

                def rotate(X):
                    if X:
                        dve.wait_ge(s_spl[1], PRIMED + i * NI + l)
                    e = T.next()
                    mark(V.tensor_tensor(qk[X][:, 0, :], e, rope_sb[:, 0, :], ALU.mult))
                    V.tensor_tensor(qk[X][:, 1, :], e, rope_sb[:, 1, :], ALU.mult).then_inc(s_mf, 1)
                    o = T.next()
                    mark(V.scalar_tensor_tensor(out=rb[X][:, 0, :], in0=o, scalar=-1.0, in1=rope_sb[:, 1, :],
                                                op0=ALU.mult, op1=ALU.mult))
                    V.tensor_tensor(rb[X][:, 1, :], o, rope_sb[:, 0, :], ALU.mult).then_inc(s_mf, 1)
                    until(k[0])
                    dve.wait_ge(s_mf, PRIMED + i * N_MISC + base + T.j)
                    link(V.tensor_tensor(qk[X][:], qk[X][:], rb[X], ALU.add))
                    split(i, l, X)

                rotate(0)
                V.tensor_copy(cT[:, 0, :], T.next()).then_inc(s_mf, 1)
                rotate(1)
                dve.wait_ge(s_pv, PRIMED + i * NI * KTS + (l - 1) * KTS)
                for h in range(TT // 2):
                    v = T.next().rearrange("p (t h d) -> p t h d", t=2, h=NH)
                    V.tensor_copy(vp[a][:, 2 * h:2 * h + 2, :, 0:DH], v).then_inc(s_mf, 1)
                dve.wait_ge(s_mf, PRIMED + i * N_MISC + base + T.j)
                dve.sem_inc(s_vp, 1)

            def route(i, a, logits):
                V.tensor_tensor(lg[:], logits, gb_bc[:].unsqueeze(1).to_broadcast([P, TT, NR]), ALU.add).then_inc(s_mf, 1)
                dve.wait_ge(s_mf, PRIMED + i * N_MISC + BASE["fb", a] + 3)
                el = lg[:, :, NGRP:NR].rearrange("p t (g e) -> p t g e", g=NGRP)
                mark(V.tensor_tensor(gmx[:], lg[:, :, 0:1], lg[:, :, 1:2], ALU.max))
                link(V.tensor_reduce(emx[:], el, AX.X, ALU.max))
                mark(V.tensor_tensor(zr[:, :, 0:NGRP], lg[:, :, 0:NGRP], gmx[:].to_broadcast([P, TT, NGRP]), ALU.subtract))
                mark(V.tensor_tensor(zr[:, :, NGRP:NR].rearrange("p t (g e) -> p t g e", g=NGRP), el,
                                     emx[:].unsqueeze(3).to_broadcast([P, TT, NGRP, EPG]), ALU.subtract))
                ready(s_zr)
                dve.wait_ge(s_ez, PRIMED + i * 2 + a + 1)
                ee = ez[:, :, NGRP:NR].rearrange("p t (g e) -> p t g e", g=NGRP)
                mark(V.tensor_reduce(esum[:], ee, AX.X, ALU.add))
                mark(V.tensor_tensor(gsum[:], ez[:, :, 0:1], ez[:, :, 1:2], ALU.add))
                mark(V.tensor_tensor(gtop[:], ez[:, :, 0:1], ez[:, :, 1:2], ALU.max))
                mark(V.tensor_tensor(gsel[:, :, 1:2], ez[:, :, 1:2], ez[:, :, 0:1], ALU.is_gt))
                link(V.tensor_copy(rank[:], rank0[:]))
                mark(V.reciprocal(esum[:], esum[:]))
                mark(V.reciprocal(gsum[:], gsum[:]))
                link(V.tensor_scalar(gsel[:, :, 0:1], gsel[:, :, 1:2], -1.0, 1.0, ALU.mult, ALU.add))
                mark(V.tensor_tensor(gtop[:], gtop[:], gsum[:], ALU.mult))
                link(V.tensor_tensor(gsel[:], gsel[:], esum[:], ALU.mult))
                link(V.tensor_tensor(gsel[:], gsel[:], gtop[:].to_broadcast([P, TT, NGRP]), ALU.mult))
                for d in range(1, EPG):
                    link(V.tensor_tensor(cmp[:, :, :, 0:EPG - d], ee[:, :, :, d:EPG], ee[:, :, :, 0:EPG - d], ALU.is_gt))
                    link(V.tensor_tensor(rank[:, :, :, 0:EPG - d], rank[:, :, :, 0:EPG - d], cmp[:, :, :, 0:EPG - d], ALU.add))
                    link(V.tensor_tensor(rank[:, :, :, d:EPG], rank[:, :, :, d:EPG], cmp[:, :, :, 0:EPG - d], ALU.subtract))
                link(V.tensor_scalar(rank[:], rank[:], 1.5, None, ALU.is_lt))
                link(V.tensor_tensor(rank[:], rank[:], ee, ALU.mult))
                link(V.tensor_tensor(we[:], rank[:], gsel[:].unsqueeze(3).to_broadcast([P, TT, NGRP, EPG]), ALU.mult))

            def stage_fa(i, a):
                base = BASE["fa", a]
                T = Tiles(i, base)
                y = src[a]
                for c in range(CT):
                    V.tensor_copy(nT[:, c, :], T.next()).then_inc(s_mf, 1)
                for h in range(TT // 2):
                    yy = y[:, 2 * h:2 * h + 2, :]
                    V.tensor_tensor(yy, yy, T.next().rearrange("p (t n) -> p t n", t=2), ALU.add).then_inc(s_mf, 1)
                dve.wait_ge(s_mf, PRIMED + i * N_MISC + base + T.j)
                statistics(i, "y", a, y)

            def norm_y(i, a):
                scaled(i, "y", a, src[a], src[a], n1_bc)
                dve.sem_inc(s_xr, 1)

            def stage_fb(i, a):
                base = BASE["fb", a]
                T = Tiles(i, base)
                y = src[a]
                for c in range(CT):
                    V.tensor_copy(cT[:, c, :], T.next()).then_inc(s_mf, 1)
                route(i, a, T.next()[:, 0:TT * 16].rearrange("p (t n) -> p t n", t=TT)[:, :, 0:NR])
                for net in range(2):
                    for j in range(HT):
                        nth = net * HT + j
                        dve.wait_ge(s_th, PRIMED + i * 4 * HT + a * 2 * HT + nth + 1)
                        if nth >= 2:
                            dve.wait_ge(s_mf, PRIMED + i * N_MISC + base + T.j)
                        V.scalar_tensor_tensor(out=uu[:, nth % 2, :], in0=th[:, nth % 2, :], scalar=1.0, in1=T.next(),
                                                    op0=ALU.add, op1=ALU.mult).then_inc(s_mf, 1)
                        dve.wait_ge(s_mf, PRIMED + i * N_MISC + base + T.j)
                        V.scalar_tensor_tensor(out=hT[:, j, :], in0=uu[:, nth % 2, :], scalar=0.5, in1=T.next(),
                                                    op0=ALU.mult, op1=ALU.mult).then_inc(s_mf, 1)
                    if net == 0:
                        for h in range(TT // 2):
                            yy = y[:, 2 * h:2 * h + 2, :]
                            V.tensor_tensor(yy, yy, T.next().rearrange("p (t n) -> p t n", t=2), ALU.add).then_inc(s_mf, 1)
                for tt in range(TT):
                    for e in range(0, NE, 2):
                        r = T.next()
                        dve.wait_ge(s_mf, PRIMED + i * N_MISC + base + T.j - 1)
                        link(V.scalar_tensor_tensor(out=y[:, tt, :], in0=r[:, 0:D], scalar=we[:, tt, e // EPG, e % EPG:e % EPG + 1],
                                                    in1=y[:, tt, :], op0=ALU.mult, op1=ALU.add))
                        e += 1
                        V.scalar_tensor_tensor(out=y[:, tt, :], in0=r[:, D:2 * D], scalar=we[:, tt, e // EPG, e % EPG:e % EPG + 1],
                                                    in1=y[:, tt, :], op0=ALU.mult, op1=ALU.add).then_inc(s_mf, 1)
                assert T.j == FB_TILES
                dve.wait_ge(s_mf, PRIMED + i * N_MISC + base + T.j)
                statistics(i, "out", a, y)
                scaled(i, "out", a, sa[a], y, n2_bc)
                mark(V.tensor_tensor(sa[a][:], sa[a][:], xin[a][:], ALU.add))
                ready(s_fin)

            def s2(i, a):
                dve.wait_ge(s_x1, PRIMED + i * 2 + a + 1)
                statistics(i, "x1", a, xin[a])

            def n1(i, a):
                dve.wait_ge(s_ldx[a], 1 + 16 + i * 16)
                statistics(i, "x", a, xin[a])

            stage = {"n1": n1, "s2": s2, "p1": stage_p1, "p2": stage_p2, "fa": stage_fa, "nf": norm_y, "fb": stage_fb}

            def row_max(i, l, p):
                q = l * PAIRS + p
                gi = q // (PAIRS // NG)
                h, t2 = p % (PAIRS // NG) // 2, p % 2
                c, bank = ring.take()
                dve.wait_ge(s_rf, PRIMED + i * N_RING + c + 1)
                V.tensor_reduce(negm[:, gi % 2, 2 * t2:2 * t2 + 2, h], ps[:, bank:bank + 2, :], AX.X, ALU.max,
                                negate=True).then_inc(s_re, 1)
                if (p + 1) % (PAIRS // NG) == 0:
                    dve.wait_ge(s_re, PRIMED + i * N_RING + c + 1)
                    m, o = negm[:, gi % 2], m2[:, gi % 2]
                    link(V.tensor_copy(o[:, :, 0, :], m))
                    mark(V.tensor_tensor(o[:, :, 1, :], m, o[:, :, 0, :], ALU.subtract))
                    ready(s_m2)

            def max_turned(i, gi):
                c, bank = ring.take()
                dve.wait_ge(s_rf, PRIMED + i * N_RING + c + 1)
                if gi >= 2:
                    dve.wait_ge(s_mrow, PRIMED + i * NI * NG * 16 * MPART + 16 * MPART * (gi - 1))
                V.tensor_copy(mTs[:, gi % 2, :], ps[:, bank, 0:L // 2].bitcast(BF16)[0:MPART * HG, :]).then_inc(s_re, 1)
                dve.wait_ge(s_re, PRIMED + i * N_RING + c + 1)
                dve.sem_inc(s_mts, 1)

            def heads_out(i, gi):
                l, g = divmod(gi, NG)
                a = l % 2
                c, bank = ring.take()
                dve.wait_ge(s_rf, PRIMED + i * N_RING + c + 1)
                o = ps[:, bank, :].rearrange("p (t h d) -> p t h d", t=TT, h=HG)
                link(V.reciprocal(rec[:], o[:, :, :, DH]))
                if l < 2:
                    link(V.tensor_scalar(rec[:], rec[:], tg[:, 0:1], None, ALU.mult))
                V.tensor_tensor(sa[a][:, :, g * HG * DH:(g + 1) * HG * DH].rearrange("p t (h d) -> p t h d", h=HG),
                                     o[:, :, :, 0:DH], rec[:].unsqueeze(3).to_broadcast([P, TT, HG, DH]), ALU.mult).then_inc(s_re, 1)
                dve.wait_ge(s_re, PRIMED + i * N_RING + c + 1)
                if l < 2:
                    dve.sem_inc(s_hd, 1)
                elif g == NG - 1:
                    dve.sem_inc(s_sa, 1)

            with dve.Fori(0, B // 2) as i:
                it[0] = i * LINKS + SETUP
                k[0] = 0
                ring = Ring()
                dve.wait_ge(s_st, PRIMED + i * 32)
                dve.wait_ge(s_mrow, PRIMED + i * NI * NG * 16 * MPART)
                for kind, a in START:
                    stage[kind](i, a)
                for p in range(LEAD):
                    row_max(i, 0, p)
                max_turned(i, 0)
                for l in range(NI):
                    for g in range(NG):
                        gi = l * NG + g
                        for s in range(STEPS):
                            if s % 2:
                                p = (g * STEPS + s) // 2 + LEAD
                                if p < PAIRS:
                                    row_max(i, l, p)
                                elif l + 1 < NI:
                                    row_max(i, l + 1, p - PAIRS)
                            if s == AT_HEADS and gi > 0:
                                heads_out(i, gi - 1)
                            if s == AT_MAX and gi + 1 < NI * NG:
                                max_turned(i, gi + 1)
                            for kind, a in HOOKS.get((l, g, s), []):
                                if kind in stage:
                                    stage[kind](i, a)
                heads_out(i, NI * NG - 1)
                for kind, a in END:
                    stage[kind](i, a)
                assert k[0] == LINKS, k[0]

        @block.tensor
        def _(pe):
            MM, TR = nc.tensor.matmul, nc.tensor.transpose
            pe.wait_ge(s_id, 4)
            pe.wait_ge(s_wn, 48)
            for j, w in enumerate((src[0], src[1], sa[0])):
                for c in range(CT):
                    for o in range(CT):
                        last = TR(ps[:, j, c * D + o * P:c * D + (o + 1) * P], w[:, o, c * P:(c + 1) * P], identf[:])
                last.then_inc(s_wt, 1)
            pe.wait_ge(s_set, 4)

            class Tiles:

                def __init__(self, i, base, units):
                    self.i, self.base, self.j = i, base, 0
                    pe.wait_ge(s_exp, PRIMED + i * NI * UNITS + units)

                def next(self):
                    if self.j >= 3:
                        self.evacuated(self.j - 2)
                    self.j += 1
                    return ps[:, MISC_BANKS[(self.j - 1) % 3], :]

                def evacuated(self, n):
                    pe.wait_ge(s_mf, PRIMED + self.i * N_MISC + self.base + n)

            def turn(T, t):
                for c in range(CT):
                    o = T.next()
                    for tt in range(TT):
                        last = TR(o[:, tt * P:(tt + 1) * P], t[:, tt, c * P:(c + 1) * P], identf[:])
                    last.then_inc(s_mt, 1)

            def product(o, terms):
                for n, (w, r) in enumerate(terms):
                    last = MM(o, w, r, start=(n == 0), stop=(n == len(terms) - 1))
                return last

            def stage_p1(i, a, T):
                pe.wait_ge(s_src, PRIMED + i * NI + a + 1)
                turn(T, src[a])
                pe.wait_ge(s_ldc, PRIMED + i * 32 + 16 * (a + 1))
                turn(T, ctxs)
                for X, r in ((0, nT), (1, cT)):
                    for o in range(CT):
                        b_ = T.next()
                        T.evacuated(2 + 2 * X)
                        product(b_, [(wT[:, X, k, o * P:(o + 1) * P], r[:, k, :]) for k in range(CT)]).then_inc(s_mt, 1)
                for h in range(TT // 2):
                    o = T.next()
                    for t in range(2):
                        tt = 2 * h + t
                        last = product(o[:, t * D:(t + 1) * D], [(cT[:, k, tt * P:(tt + 1) * P], wT[:, 2, k, :]) for k in range(CT)])
                    last.then_inc(s_mt, 1)

            def stage_p2(i, a, T):
                pe.wait_ge(s_w, 16 * N_LARGE)
                pe.wait_ge(s_src, PRIMED + i * NI + 2 + a + 1)
                turn(T, src[a])

                def halves(w, r):
                    for f in range(2):
                        o = T.next()
                        if f == 0:
                            T.evacuated(T.j - 1)
                        product(o, [(w_[:, f * P:(f + 1) * P], r_)
                                    for w_, r_ in zip(w, r)]).then_inc(s_mt, 1)

                halves([fq[:, k, :] for k in range(CT)], [nT[:, k, :] for k in range(CT)])
                product(T.next(), [(fkvc[:, k, :], nT[:, k, :]) for k in range(CT)]).then_inc(s_mt, 1)
                halves([fkv[0:DC, :]], [cT[0:DC, 0, :]])
                for h in range(TT // 2):
                    o = T.next()
                    for t in range(2):
                        tt = 2 * h + t
                        last = MM(o[:, t * D:(t + 1) * D], cT[DC:2 * DC, 0, tt * P:(tt + 1) * P], fkv[DC:2 * DC, :],
                                  start=True, stop=True)
                    last.then_inc(s_mt, 1)

            def stage_fa(i, a, T):
                pe.wait_ge(s_sa, PRIMED + i * 2 + a + 1)
                turn(T, sa[a])
                for h in range(TT // 2):
                    o = T.next()
                    T.evacuated(2)
                    for t in range(2):
                        tt = 2 * h + t
                        last = product(o[:, t * D:(t + 1) * D], [(nT[:, k, tt * P:(tt + 1) * P], fo[:, k, :]) for k in range(CT)])
                    last.then_inc(s_mt, 1)

            def stage_fb(i, a, T):
                pe.wait_ge(s_xr, PRIMED + i * 2 + a + 1)
                turn(T, src[a])
                o = T.next()
                T.evacuated(2)
                for tt in range(TT):
                    last = product(o[:, tt * 16:tt * 16 + NR], [(cT[:, k, tt * P:(tt + 1) * P], fg[:, k, :]) for k in range(CT)])
                last.then_inc(s_mt, 1)
                for net in range(2):
                    for j in range(HT):
                        for half in range(2):
                            c = half * HID + j * P
                            product(T.next(), [(fin[:, net, k, c:c + P], cT[:, k, :]) for k in range(CT)]).then_inc(s_mt, 1)
                    hidden = T.j
                    if net == 0:
                        for h in range(TT // 2):
                            o = T.next()
                            T.evacuated(hidden)
                            for t in range(2):
                                tt = 2 * h + t
                                last = product(o[:, t * D:(t + 1) * D],
                                               [(hT[:, k, tt * P:(tt + 1) * P], fout[:, k, :]) for k in range(HT)])
                            last.then_inc(s_mt, 1)
                for tt in range(TT):
                    for e in range(0, NE, 2):
                        o = T.next()
                        T.evacuated(max(hidden, T.j - 3))
                        product(o, [(hT[:, k, tt * P:(tt + 1) * P], w2[:, k, e:e + 2, :].rearrange("p e n -> p (e n)"))
                                    for k in range(HT)]).then_inc(s_mt, 1)
                assert T.j == FB_TILES

            stage = {"p1": stage_p1, "p2": stage_p2, "fa": stage_fa, "fb": stage_fb}

            def run(i, kind, a, units):
                base = BASE[(kind, a)]
                T = Tiles(i, base, units)
                stage[kind](i, a, T)
                T.evacuated(T.j)

            def ring_bank(i):
                c, bank = ring.take()
                pe.wait_ge(s_re, PRIMED + i * N_RING + max(c - 1, 0))
                return bank

            def max_pair(i, l, p):
                q = l * PAIRS + p
                gi = q // (PAIRS // NG)
                g = gi % NG
                h, t2 = p % (PAIRS // NG) // 2, p % 2
                if p % (PAIRS // NG) == 0:
                    pe.wait_ge(s_stk[g], PRIMED + (i * NI + gi // NG + 1) * 64)
                bank = ring_bank(i)
                for t in range(2):
                    tt = 2 * t2 + t
                    last = MM(ps[:, bank + t, :], qs[0:STK, g, h, tt * P:(tt + 1) * P], ks[0:STK, g, h, :],
                              start=True, stop=True)
                last.then_inc(s_rf, 1)

            def turn_max(i, gi):
                pe.wait_ge(s_m2, PRIMED + i * NI * NG + gi + 1)
                o = ps[:, ring_bank(i), 0:L // 2].bitcast(BF16)
                for tt in range(TT):
                    last = TR(o[0:MPART * HG, tt * P:(tt + 1) * P],
                              m2[:, gi % 2, tt].rearrange("p s h -> p (s h)"), identb[:])
                last.then_inc(s_rf, 1)

            def turn_heads(i, gi):
                pe.wait_ge(s_oc, PRIMED + i * NI * NG + gi + 1)
                bank = ring_bank(i)
                for tt in range(TT):
                    last = TR(ps[:, bank, tt * P:(tt + 1) * P], oT[:, tt * P:(tt + 1) * P], identf[:])
                last.then_inc(s_rf, 1)

            def values(i, gi, kt):
                l, g = divmod(gi, NG)
                kk = gi * TT + kt
                if kt == 0:
                    pe.wait_ge(s_oc, PRIMED + i * NI * NG + gi)
                    if g == 0:
                        pe.wait_ge(s_vp, PRIMED + i * NI + l + 1)
                pe.wait_ge(s_exp, PRIMED + i * NI * UNITS + HG * (kk + 1))
                for h in range(HG):
                    last = MM(ps[32 * h:32 * h + VM, 6, :], vp[l % 2][:, kt, g * HG + h, :], prob[:, kk % PROB_SLOTS, h, :],
                              start=(kt == 0), stop=(kt == TT - 1))
                last.then_inc(s_pv, 1)

            with pe.Fori(0, B // 2) as i:
                ring = Ring()
                for kind, a in START:
                    if kind in stage:
                        run(i, kind, a, 0)
                for p in range(LEAD):
                    max_pair(i, 0, p)
                turn_max(i, 0)
                for l in range(NI):
                    for g in range(NG):
                        gi = l * NG + g
                        for s in range(STEPS):
                            u = gi * STEPS + s
                            kt, h = divmod(s, HG)
                            if s == 0:
                                pe.wait_ge(s_mrow, PRIMED + (i * NI * NG + gi + 1) * 16 * MPART)
                            if u >= 3:
                                pe.wait_ge(s_exp, PRIMED + i * NI * UNITS + u - 2)
                            MM(ps[:, SCORE_BANKS[u % 3], :], ks[:, g, h, kt * P:(kt + 1) * P], qs[:, g, h, :],
                               start=True, stop=True).then_inc(s_sT, 1)
                            if s % 2:
                                p = (g * STEPS + s) // 2 + LEAD
                                if p < PAIRS:
                                    max_pair(i, l, p)
                                elif l + 1 < NI:
                                    max_pair(i, l + 1, p - PAIRS)
                            if s % HG == HG - 1 and (kt or gi):
                                values(i, *((gi, kt - 1) if kt else (gi - 1, TT - 1)))
                            if s == AT_HEADS and gi > 0:
                                turn_heads(i, gi - 1)
                            if s == AT_MAX and gi + 1 < NI * NG:
                                turn_max(i, gi + 1)
                            for kind, a in HOOKS.get((l, g, s), []):
                                if kind in stage:
                                    run(i, kind, a, u + 1)
                values(i, NI * NG - 1, TT - 1)
                turn_heads(i, NI * NG - 1)
                for kind, a in END:
                    if kind in stage:
                        run(i, kind, a, NI * UNITS)


PRIMED = 1
N_SMALL, N_LARGE = 8, 21
LINKS = 232
POOL_LINKS = 68


def rope_table(L, dh, nh):
    inv = (np.float32(1.0) / np.float32(10000.0) ** (np.arange(0, dh, 2, dtype=np.float32) / np.float32(dh))).astype(np.float32)
    ang = np.arange(L, dtype=np.float32)[:, None] * inv[None, :]
    t = np.stack([np.cos(ang), np.sin(ang)]).astype(np.float32)
    return np.ascontiguousarray(np.repeat(t.transpose(0, 2, 1), nh, axis=1))


_INS = ["x", "ctx_1024", "g_xattn", "g_ffn", "L0_xattn_wq", "L0_xattn_bq", "L0_xattn_wk", "L0_xattn_bk", "L0_xattn_wv",
        "L0_xattn_bv", "L0_ffn_Wq", "L0_ffn_Wk_c", "L0_ffn_Wv_c", "L0_ffn_Wk", "L0_ffn_Wv", "L0_ffn_Wo", "L0_ffn_W_shared_in",
        "L0_ffn_W_shared_out", "L0_ffn_W1_shared", "L0_ffn_W2_experts", "L0_ffn_Wg_gate", "L0_ffn_We_gate",
        "L0_ffn_group_bias", "L0_ffn_expert_bias", "L0_ffn_norm1_w", "L0_ffn_norm2_w"]


def kernel(**inputs):
    import concourse.bacc as _bacc
    from concourse.bass_utils import run_bass_kernel_spmd as _run

    nc = _bacc.Bacc("TRN2", target_bir_lowering=False, num_devices=1)
    arrays, args = {}, []
    given = {name: np.ascontiguousarray(inputs[name]) for name in _INS}
    B, L, D = given["x"].shape
    given["rope"] = rope_table(L, 16, 16)
    for name, a in given.items():
        arrays[f"in_{name}_dram"] = a
        args.append(nc.dram_tensor(f"in_{name}_dram", a.shape, mybir.dt.from_np(a.dtype), kind="ExternalInput").ap())
    args.append(nc.dram_tensor("out_dram", (B, L, D), F32, kind="ExternalOutput").ap())
    flamingo_block(nc, *args)
    r = _run(nc, [arrays], core_ids=[0])
    return r.results[0]["out_dram"]
```

```python
from contextlib import ExitStack, nullcontext

import numpy as np
import concourse.bass as bass
from concourse import mybir

F32 = mybir.dt.float32
BF16 = mybir.dt.bfloat16
ALU = mybir.AluOpType
ACT = mybir.ActivationFunctionType
AX = mybir.AxisListType

P = 128
HG = 4
NTERM = 6
NPART = 3
MPART = 2
Q_PART = [0, 0, 0, 1, 1, 2]
K_PART = [0, 1, 2, 0, 1, 0]
LEAD = 12
PROB_SLOTS = 3
AT_COPY, AT_HEADS, AT_MAX, AT_ROWS = 4, 8, 9, 11
SCORE_BANKS = [0, 1, 7]
MISC_BANKS = SCORE_BANKS


def flamingo_block(nc, x, ctx_in, g_xattn, g_ffn, wq, bq, wk, bk, wv, bv,
                   f_wq, f_wkc, f_wvc, f_wk, f_wv, f_wo, f_in, f_out, f_w1, f_w2,
                   f_gg, f_ge, f_gb, f_eb, n1, n2, rope, out):
    B, L, D = x.shape
    NH = 16
    DH = D // NH
    TT = L // P
    CT = D // P
    NG = NH // HG
    HID = f_out.shape[0]
    HT = HID // P
    NE = f_w2.shape[0]
    NGRP = f_gg.shape[1]
    EPG = NE // NGRP
    NR = NGRP + NE
    DC = f_wkc.shape[1]
    STK = NTERM * DH
    KROWS = STK + MPART
    NI = 4
    PAIRS = NH * TT // 2
    UNITS = NH * TT
    KTS = NG * TT
    STEPS = UNITS // NG
    SCR = [16 * 5, 16 * 3]
    SC = 1.0 / float(DH) ** 0.5
    assert (L, D, DH, CT, TT, DC, EPG) == (512, 256, 16, 2, 4, 64, 4)

    NB = B // 2
    OWNER = {"p1": "A" * 8 + "VV", "p2": "AA" + "VV" + "A" + "VV" + "AA", "fa": "AA" + "VV",
             "fb": "AA" + "V" * (1 + 2 * 2 * HT + 2 + TT * NE // 2)}
    REST = "rest"
    HOOKS = {("lead", 4): [("fa", 1, -1)], ("lead", 11): [("nf", 1, -1)], (0, 0, 0): [("fb", 1, -1)],
             (0, 0, 8): [("no", 1, -1)],
             (0, 1, 1): [("s1", 1, REST)], (0, 1, 6): [("n1", 1, REST)], (0, 1, 8): [("m1", 1, REST)],
             (0, 1, 11): [("p1", 1, REST)], (0, 1, 13): [("q1", 1, REST)],
             (1, 0, 11): [("s2", 0, 0)], (1, 1, 3): [("n2", 0, 0)], (1, 1, 5): [("m2", 0, 0)], (1, 1, 7): [("p2", 0, 0)], (1, 1, 9): [("q2", 0, 0)],
             (2, 0, 11): [("s2", 1, 0)], (2, 1, 3): [("n2", 1, 0)], (2, 1, 5): [("m2", 1, 0)], (2, 1, 7): [("p2", 1, 0)], (2, 1, 9): [("q2", 1, 0)],
             (3, 0, 13): [("fa", 0, 0)], (3, 1, 4): [("nf", 0, 0)], (3, 1, 7): [("fb", 0, 0)],
             (3, 1, 15): [("no", 0, 0)], (3, 2, 5): [("s1", 0, 1)], (3, 2, 9): [("n1", 0, 1)], (3, 2, 12): [("m1", 0, 1)], (3, 2, 15): [("p1", 0, 1)],
             (3, 3, 1): [("q1", 0, 1)]}
    END = [("fa", 1), ("nf", 1), ("fb", 1), ("no", 1)]
    N_TURN = NI * NG
    N_RING = NI * PAIRS + N_TURN
    FB = len(OWNER["fb"])
    NORMS = ["x", "x1", "y", "out"]
    NN = len(NORMS)
    VM = DH + 1

    es = ExitStack()
    with es:
        def sb(name, shape, dt):
            return es.enter_context(nc.sbuf_tensor(name, shape, dt))

        def sem(name):
            return es.enter_context(nc.semaphore(name))

        wT = sb("wT", [P, 3, CT, D], F32)
        fq = sb("fq", [P, CT, D], F32)
        fkvc = sb("fkvc", [P, CT, 2 * DC], F32)
        fkv = sb("fkv", [P, D], F32)
        fo = sb("fo", [P, CT, D], F32)
        fin = sb("fin", [P, 2, CT, 2 * HID], F32)
        fout = sb("fout", [P, HT, D], F32)
        w2 = sb("w2", [P, HT, NE, D], F32)
        fg = sb("fg", [P, CT, NR], F32)
        bqk = sb("bqk", [P, 2, CT], F32)
        bv_bc = sb("bv_bc", [P, D], F32)
        n1_bc = sb("n1_bc", [P, D], F32)
        n2_bc = sb("n2_bc", [P, D], F32)
        gb_bc = sb("gb_bc", [P, NR], F32)
        gates = sb("gates", [P, 2], F32)
        tg = sb("tg", [P, 2], F32)
        rope_sb = sb("rope_sb", [P, 2, L], F32)
        identf = sb("identf", [P, P], F32)
        identb = sb("identb", [P, P], BF16)
        rank0 = sb("rank0", [P, TT, NGRP, EPG], F32)
        xin = [sb(f"xin{i}", [P, TT, D], F32) for i in range(2)]
        ctxs = sb("ctxs", [P, TT, D], F32)
        src = [sb(f"src{i}", [P, TT, D], F32) for i in range(2)]
        sa = [sb(f"sa{i}", [P, TT, D], F32) for i in range(2)]
        nT = sb("nT", [P, CT, L], F32)
        cT = sb("cT", [P, CT, L], F32)
        qk = [sb(f"qk{i}", [P, 2, L], F32) for i in range(2)]
        hT = sb("hT", [P, HT, L], F32)
        rb = [hT[:, 2 * X:2 * X + 2, :] for X in range(2)]
        parts = [sb(f"parts{i}", [P, NPART, 2, L], BF16) for i in range(2)]
        qs = sb("qs", [KROWS, NG, HG, L], BF16)
        ks = sb("ks", [KROWS, NG, HG, L], BF16)
        vp = [sb(f"vp{i}", [P, TT, NH, VM], F32) for i in range(2)]
        prob = sb("prob", [P, PROB_SLOTS, HG, L], F32)
        oT = sb("oT", [P, L], F32)
        negm = sb("negm", [P, 2, TT, HG], F32)
        m2 = sb("m2", [P, 2, TT, MPART, HG], BF16)
        mTs = sb("mTs", [MPART * HG, 2, L], BF16)
        rec = sb("rec", [P, TT, HG], F32)
        bst = sb("bst", [P, NN, TT, 6], F32)
        mean = sb("mean", [P, TT], F32)
        mdif = sb("mdif", [P, TT], F32)
        nvar = sb("nvar", [P, TT], F32)
        scale_ = sb("scale", [P, 2 * NN, TT], F32)
        shift_ = sb("shift", [P, 2 * NN, TT], F32)
        mhalf = sb("mhalf", [P, TT], F32)
        th = qk[0]
        uu = ctxs[:].rearrange("p (j t) c -> p j (t c)", j=2)
        lg = sb("lg", [P, TT, NR], F32)
        gmx = sb("gmx", [P, TT, 1], F32)
        emx = sb("emx", [P, TT, NGRP], F32)
        zr = sb("zr", [P, TT, NR], F32)
        ez = sb("ez", [P, TT, NR], F32)
        gsum = sb("gsum", [P, TT, 1], F32)
        gtop = sb("gtop", [P, TT, 1], F32)
        esum = sb("esum", [P, TT, NGRP], F32)
        gsel = sb("gsel", [P, TT, NGRP], F32)
        rank = sb("rank", [P, TT, NGRP, EPG], F32)
        cmp = sb("cmp", [P, TT, NGRP, EPG], F32)
        we = sb("we", [P, TT, NGRP, EPG], F32)

        ps = es.enter_context(nc.psum_tensor("ps", [P, 8, L], F32))
        scrq = nc.dram_tensor("scrq", [2, NTERM, DH * NH, L], BF16, kind="Internal").ap()
        scrk = nc.dram_tensor("scrk", [2, NPART, DH * NH, L], BF16, kind="Internal").ap()

        s_w = sem("weights_loaded")
        s_wl = sem("ffn_weights_loaded")
        s_ws = sem("small_weights_loaded")
        s_wn = sem("xattn_weights_loaded")
        s_id = sem("identity_steps")
        s_wt = sem("weight_transposed")
        s_wtd = sem("weight_copied")
        s_set = sem("setup_done")
        s_tg = sem("gate_tanh")
        s_ldx = [sem(f"x_loaded{i}") for i in range(2)]
        s_ldc = sem("ctx_loaded")
        s_src = sem("normed_ready")
        s_mt = {n: sem(f"{n}_tile_full") for n in OWNER}
        s_mf = {n: sem(f"{n}_tile_emptied_by_dve") for n in OWNER}
        s_ma = {n: sem(f"{n}_tile_emptied_by_act") for n in OWNER}
        s_p0 = [sem(f"first_part_ready{i}") for i in range(2)]
        s_r0 = [sem(f"first_rest_ready{i}") for i in range(2)]
        s_p1 = [sem(f"second_part_ready{i}") for i in range(2)]
        s_spl = [sem(f"parts_ready{i}") for i in range(2)]
        s_bst = {n: sem(f"{n}_row_statistics") for n in NORMS}
        s_ny = {n: sem(f"{n}_row_scale_ready") for n in NORMS}
        s_hd = sem("heads_ready")
        s_x1 = sem("x1_ready")
        s_pool = {n: sem(f"pool_chain_{n}") for n in POOL_LINKS}
        s_scr = [sem(f"scratch_written{i}") for i in range(2)]
        s_stk = [sem(f"stack_loaded{g}") for g in range(NG)]
        s_vp = sem("values_ready")
        s_rf = sem("ring_full")
        s_re = sem("ring_emptied")
        s_m2 = sem("maximum_parts")
        s_mtf = sem("maximum_turned")
        s_mts = sem("turned_maximum_copied")
        s_mrow = sem("maximum_rows")
        s_sT = sem("score_full")
        s_exp = sem("exp_done")
        s_pv = sem("value_product")
        s_oc = sem("value_copied")
        s_sa = sem("self_attention_ready")
        s_th = sem("tanh_ready")
        s_xr = sem("block_normed")
        s_zr = sem("router_shifted")
        s_ez = sem("router_exp")
        s_fin = sem("result_ready")
        s_st = [sem(f"result_stored{i}") for i in range(2)]
        s_dve = {n: sem(f"dve_chain_{n}".replace(" ", "_")) for n in LINKS}
        s_ini = sem("dve_setup_chain")
        s_one = sem("ones_ready")
        s_held = sem("waits_passed")


        LOOPED = [*s_ldx, s_ldc, s_src, *s_mt.values(), *s_mf.values(), *s_ma.values(), *s_p0, *s_r0, *s_p1, *s_spl,
                  *s_bst.values(), *s_ny.values(), s_hd, s_x1, *s_scr, *s_stk, s_vp, s_rf, s_re, s_m2, s_mtf, s_mts, s_mrow,
                  s_sT, s_exp, s_pv, s_oc, s_sa, s_th, s_xr, s_zr, s_ez, s_fin, *s_st, *s_pool.values(), *s_dve.values()]

        def only(eng, i, d):
            if d == 0:
                return nullcontext()
            eng.sem_inc(s_held, 1)
            return eng.If(i < NB - 1) if d == 1 else eng.If(i > 0)

        def pair(i, d):
            return i if d == REST else i + d

        def emptied(kind, who, n):
            return OWNER[kind][:n].count(who)

        block = es.enter_context(nc.Block())

        def turned_heads():
            n, after = LEAD, []
            for gi in range(NI * NG):
                for s in range(STEPS):
                    n += s % 2 and (gi * STEPS + s) // 2 + LEAD < NI * PAIRS
                    if s == AT_HEADS and gi > 0:
                        n += 1
                        after.append(n)
            assert n + 1 == N_RING and N_RING % 2 == 0
            return after

        turned = turned_heads()

        SLOTS = [("turned", 0)]
        for u in range(NI * UNITS):
            SLOTS.append(("unit", u))
            if u % STEPS == AT_MAX and u // STEPS + 1 < NI * NG:
                SLOTS.append(("turned", u // STEPS + 1))

        def slots_after(u):
            n = SLOTS.index(("unit", u)) + 1
            return n + (n < len(SLOTS) and SLOTS[n][0] == "turned")

        def misc_bank(first, t):
            return ps[:, MISC_BANKS[(first + t) % 3], :]

        def score_bank(kind, n):
            return ps[:, SCORE_BANKS[SLOTS.index((kind, n)) % 3], :]

        class Ring:
            n = 0

            def take(self):
                self.n += 1
                return self.n - 1, 2 + 2 * ((self.n - 1) % 2)

        @block.sync
        def _(sp):
            sp.dma_start(xin[0][:], x[0:1].rearrange("b (t p) c -> p (b t) c", p=P)).then_inc(s_ldx[0], 16)
            for s_, d_ in ((src[0], wq), (src[1], wk), (sa[0], wv)):
                sp.dma_start(s_[:, 0:CT, :], d_.rearrange("(o p) c -> p o c", p=P)).then_inc(s_wn, 16)
            sp.dma_start(ctxs[:], ctx_in[0:1].rearrange("b (t p) c -> p (b t) c", p=P)).then_inc(s_ldc, 16)
            sp.dma_start(xin[1][:], x[1:2].rearrange("b (t p) c -> p (b t) c", p=P)).then_inc(s_ldx[1], 16)
            small = (
                *((bqk[:, X, o:o + 1], b_.rearrange("(h o d) -> o d h", h=NH, o=2)[o]) for X, b_ in ((0, bq), (1, bk)) for o in range(2)),
                (bv_bc[:], bv.unsqueeze(0).to_broadcast([P, D])),
                (gates[:, 0:1], g_xattn.unsqueeze(0).to_broadcast([P, 1])),
                (gates[:, 1:2], g_ffn.unsqueeze(0).to_broadcast([P, 1])),
                (n2_bc[:], n2.unsqueeze(0).to_broadcast([P, D])),
                (hT[:, 0, :].rearrange("p (k n) -> p k n", k=CT), f_wq.rearrange("(k p) n -> p k n", p=P)),
                (hT[0:DC, 1, 0:D], f_wk),
            )
            assert len(small) == N_SMALL
            for d_, s_ in small:
                sp.dma_start(d_, s_, allow_slow_non_contiguous=True).then_inc(s_ws, 16)
            large = [
                (rope_sb[:], rope.rearrange("s p t -> p s t")),
                (fkvc[:, :, 0:DC], f_wkc.rearrange("(k p) n -> p k n", p=P)),
                (fkvc[:, :, DC:2 * DC], f_wvc.rearrange("(k p) n -> p k n", p=P)),
                (fkv[DC:2 * DC, :], f_wv),
                (fo[:], f_wo.rearrange("(k p) n -> p k n", p=P)),
                (n1_bc[:], n1.unsqueeze(0).to_broadcast([P, D])),
                (gb_bc[:, 0:NGRP], f_gb.unsqueeze(0).to_broadcast([P, NGRP])),
                (gb_bc[:, NGRP:NR], f_eb.unsqueeze(0).to_broadcast([P, NE])),
                (fg[:, :, 0:NGRP], f_gg.rearrange("(k p) n -> p k n", p=P)),
                (fg[:, :, NGRP:NR], f_ge.rearrange("(k p) n -> p k n", p=P)),
            ]
            assert len(large) == N_LARGE
            for d_, s_ in large:
                sp.dma_start(d_, s_).then_inc(s_w, 16)
            sp.wait_ge(s_ma["p1"], PRIMED + 4)
            sp.dma_start(ctxs[:], ctx_in[1:2].rearrange("b (t p) c -> p (b t) c", p=P)).then_inc(s_ldc, 16)

            def stack(i, l, first=False):
                par = l % 2
                for g in range(NG):
                    sp.wait_ge(s_stk[g], PRIMED + i * NI * 64 + max(l - 1, 0) * 64)
                    sp.sem_inc(s_held, 1)

                def put(X, part, ready):
                    sp.wait_ge(ready[X], PRIMED + i * NI + l + 1)
                    sp.sem_inc(s_held, 1)
                    p_ = parts[X][:, part]
                    if X or Q_PART.count(part) == 1:
                        d_ = (scrk[par, part] if X else scrq[par, Q_PART.index(part)]).rearrange("(o p) t -> p o t", p=P)
                        sp.dma_start(d_, p_).then_inc(s_scr[X], 16)
                        return
                    r = Q_PART.index(part)
                    n = Q_PART.count(part)
                    for o in range(2):
                        d_ = scrq[par, r:r + n, o * P:(o + 1) * P].rearrange("r p t -> p r t")
                        sp.dma_start(d_, p_[:, o, :].unsqueeze(1).to_broadcast([P, n, L])).then_inc(s_scr[0], 16)

                for part, ready in enumerate((s_p0, s_p1, s_spl)):
                    put(0, part, ready)
                    put(1, part, ready)
                for X in range(2):
                    sp.wait_ge(s_scr[X], PRIMED + (i * NI + l + 1) * SCR[X])
                    sp.sem_inc(s_held, 1)
                for g in range(NG):
                    if not first:
                        sp.wait_ge(s_sT, PRIMED + (i * NI + l - 1) * UNITS + (g + 1) * STEPS)
                        sp.sem_inc(s_held, 1)
                    h_ = slice(g * HG, (g + 1) * HG)
                    def heads(scr, n):
                        return scr[par, 0:n].rearrange("r (d h) t -> (r d) h t", h=NH)[:, h_]

                    sp.dma_start(qs[0:STK, g], heads(scrq, NTERM)).then_inc(s_stk[g], 16)
                    row = 0
                    for n in range(NPART, 0, -1):
                        sp.dma_start(ks[row:row + n * DH, g], heads(scrk, n)).then_inc(s_stk[g], 16)
                        row += n * DH

            def load_x(b_, a):
                sp.dma_start(xin[a][:], x[b_].rearrange("b (t p) c -> p (b t) c", p=P)).then_inc(s_ldx[a], 16)

            def load_ctx(b_):
                sp.dma_start(ctxs[:], ctx_in[b_].rearrange("b (t p) c -> p (b t) c", p=P)).then_inc(s_ldc, 16)

            def store(b_, a):
                sp.dma_start(out[b_].rearrange("b (t p) c -> p (b t) c", p=P), sa[a][:]).then_inc(s_st[a], 16)

            def within(b_, why):
                return bass.ds(nc.s_assert_within(b_, 0, B - 1, skip_runtime_bounds_check_because=why), 1)

            stack(0, 0, first=True)
            late = [
                (fin[:, 0], f_in.rearrange("(k p) n -> p k n", p=P)),
                (fin[:, 1], f_w1.rearrange("(k p) n -> p k n", p=P)),
                (fout[:], f_out.rearrange("(k p) n -> p k n", p=P)),
            ] + [(w2[:, :, e, :], f_w2[e].rearrange("(k p) n -> p k n", p=P)) for e in range(NE)]
            assert len(late) == N_LATE

            def load_late(n, unit):
                sp.wait_ge(s_sT, PRIMED + unit)
                d_, s_ = late[n]
                sp.dma_start(d_, s_).then_inc(s_wl, 16)

            for n in range(5):
                load_late(N_LATE - 1 - n, 2 + 3 * n)
            stack(0, 1)
            for n in range(N_LATE - 5):
                load_late(n, UNITS + 3 * n)
            with sp.Fori(0, NB) as i:
                sp.wait_ge(s_fin, PRIMED + i * 2)
                sp.sem_inc(s_held, 1)
                with sp.If(i > 0):
                    load_x(bass.ds(i * 2 + 1, 1), 1)
                    store(within(i * 2 - 1, "i > 0 here"), 1)
                    sp.wait_ge(s_ma["p1"], PRIMED + i * 2 * emptied("p1", "A", 10) + 4)
                    sp.sem_inc(s_held, 1)
                    sp.wait_ge(s_mf["fb"], PRIMED + i * 2 * emptied("fb", "V", FB))
                    sp.sem_inc(s_held, 1)
                    load_ctx(bass.ds(i * 2 + 1, 1))
                    stack(i, 1)
                for l in range(2, NI):
                    stack(i, l)
                sp.wait_ge(s_fin, PRIMED + i * 2 + 1)
                sp.sem_inc(s_held, 1)
                with sp.If(i < NB - 1):
                    load_x(within(i * 2 + 2, "i < NB - 1 here"), 0)
                    load_ctx(within(i * 2 + 2, "i < NB - 1 here"))
                store(bass.ds(i * 2, 1), 0)
                with sp.If(i < NB - 1):
                    stack(i + 1, 0)
            sp.wait_ge(s_fin, PRIMED + B)
            store(slice(B - 1, B), 1)
            for a in range(2):
                sp.wait_ge(s_st[a], PRIMED + 16 * NB)

        @block.gpsimd
        def _(pool):
            k = [0]
            chain = [None, 0]

            def enter(kind, n):
                chain[:] = s_pool[kind], n * POOL_LINKS[kind]
                k[0] = 0

            def leave(kind):
                assert k[0] == POOL_LINKS[kind], (kind, k[0])

            def link(ins):
                k[0] += 1
                ins.then_inc(chain[0], 1)
                pool.wait_ge(chain[0], PRIMED + chain[1] + k[0])
                pool.sem_inc(s_held, 1)

            for s_ in LOOPED:
                pool.sem_inc(s_, PRIMED)
            pool.sem_inc(s_set, 1)
            pool.memset(identf[:], 0.0).then_inc(s_id, 1)
            pool.memset(identb[:], 0.0).then_inc(s_id, 1)
            pool.wait_ge(s_id, 2)
            for m in (identf, identb):
                pool.affine_select(out=m[:], in_=m[:], compare_op=ALU.not_equal, fill=1.0, base=0,
                                   pattern=[[-1, P]], channel_multiplier=1).then_inc(s_id, 1)

            pool.memset(mhalf[:], -0.5).then_inc(s_set, 1)

            def row_scale(j, kind, a):
                e = NORMS.index(kind)
                layer = kind in ("x", "x1")
                st = bst[:, e]
                sc = scale_[:, 2 * e + a]
                enter(kind, 2 * j + a)
                pool.wait_ge(s_bst[kind], PRIMED + 2 * j + a + 1)
                pool.tensor_tensor(mdif[:], st[:, :, 1], st[:, :, 4], ALU.subtract)
                pool.tensor_tensor(mean[:], st[:, :, 1], st[:, :, 4], ALU.add)
                link(pool.tensor_tensor(nvar[:], st[:, :, 2], st[:, :, 5], ALU.add))
                pool.tensor_tensor(mdif[:], mdif[:], mdif[:], ALU.mult)
                pool.tensor_scalar(mean[:], mean[:], -0.5, None, ALU.mult)
                link(pool.tensor_scalar(nvar[:], nvar[:], 1.0 / D, 1e-5 if layer else 1e-6, ALU.mult, ALU.add))
                link(pool.tensor_scalar(mdif[:], mdif[:], 0.25, None, ALU.mult))
                link(pool.tensor_tensor(nvar[:], nvar[:], mdif[:], ALU.add))
                if not layer:
                    link(pool.tensor_tensor(mdif[:], mean[:], mean[:], ALU.mult))
                    link(pool.tensor_tensor(nvar[:], nvar[:], mdif[:], ALU.add))
                link(pool.tensor_tensor(sc, nvar[:], mhalf[:], ALU.pow))
                if layer:
                    link(pool.tensor_tensor(shift_[:, 2 * e + a], mean[:], sc, ALU.mult))
                pool.sem_inc(s_ny[kind], 1)
                leave(kind)

            def split(n):
                enter("split", n - 1)
                pool.wait_ge(s_p0[0], PRIMED + n + 1)
                pool.sem_inc(s_held, 1)
                link(pool.tensor_tensor(qk[0][:], qk[0][:], parts[0][:, 0], ALU.subtract))
                pool.sem_inc(s_r0[0], 1)
                for X in range(2):
                    pool.wait_ge(s_p1[X], PRIMED + n + 1)
                    pool.sem_inc(s_held, 1)
                    link(pool.tensor_tensor(parts[X][:, 2], qk[X][:], parts[X][:, 1], ALU.subtract))
                    pool.sem_inc(s_spl[X], 1)
                leave("split")

            def add_heads(i, gi):
                g = gi % NG
                xs = xin[gi // NG][:, :, g * HG * DH:(g + 1) * HG * DH]
                enter("add", i * 2 * NG + gi)
                pool.wait_ge(s_hd, PRIMED + i * 2 * NG + gi + 1)
                pool.sem_inc(s_held, 1)
                heads = sa[gi // NG][:, :, g * HG * DH:(g + 1) * HG * DH]
                link(pool.tensor_scalar(heads, heads, tg[:, 0:1], None, ALU.mult))
                link(pool.tensor_tensor(xs, xs, heads, ALU.add))
                if g == NG - 1:
                    pool.sem_inc(s_x1, 1)
                leave("add")

            stage = {"s1": lambda j, a: row_scale(j, "x", a), "p1": lambda j, a: split(j * NI + a),
                     "s2": lambda j, a: row_scale(j, "x1", a), "p2": lambda j, a: split(j * NI + 2 + a),
                     "fa": lambda j, a: row_scale(j, "y", a), "fb": lambda j, a: row_scale(j, "out", a)}
            stage["s1"](0, 0)
            stage["s1"](0, 1)
            pool.memset(ks[STK:KROWS], 1.0).then_inc(s_one, 1)
            pool.wait_ge(s_one, 1)
            pool.sem_inc(s_held, 1)
            stage["p1"](0, 1)
            with pool.Fori(0, NB) as i:
                for p in range(LEAD):
                    for kind, a, d in HOOKS.get(("lead", p), []):
                        if kind in stage:
                            with only(pool, i, d):
                                stage[kind](pair(i, d), a)
                for l in range(NI):
                    for g in range(NG):
                        gi = l * NG + g
                        for s in range(STEPS):
                            if s == AT_HEADS and 0 < gi <= 2 * NG:
                                add_heads(i, gi - 1)
                            for kind, a, d in HOOKS.get((l, g, s), []):
                                if kind in stage:
                                    with only(pool, i, d):
                                        stage[kind](pair(i, d), a)
            for kind, a in END:
                if kind in stage:
                    stage[kind](NB - 1, a)

        @block.scalar
        def _(act):
            act.wait_ge(s_ws, 16 * N_SMALL)
            nc.scalar.activation(tg[:], gates[:], ACT.Tanh).then_inc(s_tg, 1)

            def copy_values(i, gi):
                act.wait_ge(s_pv, PRIMED + i * NI * KTS + TT * (gi + 1))
                if gi:
                    act.wait_ge(s_rf, PRIMED + i * N_RING + turned[gi - 1])
                nc.scalar.activation(oT[:], ps[:, 6, :], ACT.Copy).then_inc(s_oc, 1)

            def max_turned(i, gi):
                act.wait_ge(s_mtf, PRIMED + i * NI * NG + gi + 1)
                act.wait_ge(s_mrow, PRIMED + (i * NI * NG + max(gi - 1, 0)) * 16 * MPART)
                nc.scalar.activation(mTs[:, gi % 2, :], score_bank("turned", gi)[:, 0:L // 2].bitcast(BF16)[0:MPART * HG, :],
                                     ACT.Copy).then_inc(s_mts, 1)

            def max_rows(i, gi):
                act.wait_ge(s_mts, PRIMED + i * NI * NG + gi + 1)
                for t in range(MPART):
                    act.dma_start(qs[STK + t:STK + t + 1, gi % NG, :, :],
                                  mTs[t * HG:(t + 1) * HG, gi % 2, :]).then_inc(s_mrow, 16)

            def normalise(j, kind, a, half):
                e = 2 * NORMS.index(kind) + a
                act.wait_ge(s_ny[kind], PRIMED + 2 * j + a + 1)
                for tt in (2 * half, 2 * half + 1):
                    last = nc.scalar.activation(src[a][:, tt, :], xin[a][:, tt, :], ACT.Identity,
                                                bias=shift_[:, e, tt:tt + 1], scale=scale_[:, e, tt:tt + 1])
                last.then_inc(s_src, 1)

            class Tiles:

                def __init__(self, kind, n):
                    self.kind, self.full, self.own = kind, n * len(OWNER[kind]), n * emptied(kind, "A", 99)

                def tile(self, t):
                    act.wait_ge(s_mt[self.kind], PRIMED + self.full + t + 1)
                    return misc_bank(first[0], t)

                def emptied(self, t):
                    act.wait_ge(s_ma[self.kind], PRIMED + self.own + emptied(self.kind, "A", t))

            first = [0]

            def project_cross(j, a):
                T = Tiles("p1", 2 * j + a)
                for c in range(2 * CT):
                    nc.scalar.activation((nT, cT)[c // CT][:, c % CT, :], T.tile(c), ACT.Copy).then_inc(s_ma["p1"], 1)
                for X in range(2):
                    act.wait_ge(s_spl[X], PRIMED + j * NI + a)
                    for o in range(CT):
                        nc.scalar.activation(qk[X][:, o, :], T.tile(4 + 2 * X + o), ACT.Identity,
                                             bias=bqk[:, X, o:o + 1]).then_inc(s_ma["p1"], 1)
                    T.emptied(6 + 2 * X)
                    act.wait_ge(s_scr[X], PRIMED + (j * NI + a) * SCR[X])
                    nc.scalar.activation(parts[X][:, 0], qk[X][:], ACT.Copy).then_inc(s_p0[X], 1)
                if not (isinstance(j, int) and a == 0):
                    second_part(j * NI + a, 0)

            def second_part(n, X):
                act.wait_ge(s_r0[X], PRIMED + n + 1)
                nc.scalar.activation(parts[X][:, 1], qk[X][:], ACT.Copy).then_inc(s_p1[X], 1)

            def project_self(j, a):
                T = Tiles("p2", 2 * j + a)
                for c in range(CT):
                    nc.scalar.activation(nT[:, c, :], T.tile(c), ACT.Copy).then_inc(s_ma["p2"], 1)
                nc.scalar.activation(cT[:, 0, :], T.tile(4), ACT.Copy).then_inc(s_ma["p2"], 1)
                act.wait_ge(s_pv, PRIMED + (j * NI + a + 1) * KTS)
                for h in range(TT // 2):
                    v = T.tile(7 + h).rearrange("p (t h d) -> p t h d", t=2, h=NH)
                    nc.scalar.activation(vp[a][:, 2 * h:2 * h + 2, :, 0:DH], v, ACT.Copy).then_inc(s_ma["p2"], 1)
                T.emptied(9)
                act.sem_inc(s_vp, 1)
                second_part(j * NI + 2 + a, 0)

            def turned_attention(j, a):
                T = Tiles("fa", 2 * j + a)
                for c in range(CT):
                    nc.scalar.activation(nT[:, c, :], T.tile(c), ACT.Copy).then_inc(s_ma["fa"], 1)

            def ffn(j, a):
                T = Tiles("fb", 2 * j + a)
                for c in range(CT):
                    nc.scalar.activation(cT[:, c, :], T.tile(c), ACT.Copy).then_inc(s_ma["fb"], 1)
                act.wait_ge(s_zr, PRIMED + 2 * j + a + 1)
                nc.scalar.activation(ez[:], zr[:], ACT.Exp).then_inc(s_ez, 1)
                for net in range(2):
                    for n in range(HT):
                        t = 3 + net * (2 * HT + 2) + 2 * n
                        nth = net * HT + n
                        if nth >= 2:
                            tp = t - 4 if n >= 2 else t - 6
                            act.wait_ge(s_mf["fb"], PRIMED + (2 * j + a) * emptied("fb", "V", FB) + emptied("fb", "V", tp + 1))
                        nc.scalar.activation(th[:, nth % 2, :], T.tile(t), ACT.Tanh, scale=0.5).then_inc(s_th, 1)

            stage = {"n1": lambda j, a: normalise(j, "x", a, 0), "m1": lambda j, a: normalise(j, "x", a, 1),
                     "n2": lambda j, a: normalise(j, "x1", a, 0), "m2": lambda j, a: normalise(j, "x1", a, 1),
                     "p1": project_cross, "q1": lambda j, a: second_part(j * NI + a, 1),
                     "p2": project_self, "q2": lambda j, a: second_part(j * NI + 2 + a, 1), "fa": turned_attention, "fb": ffn}
            act.wait_ge(s_wt, 3)
            stage["n1"](0, 0)
            stage["m1"](0, 0)
            stage["p1"](0, 0)
            stage["n1"](0, 1)
            stage["m1"](0, 1)
            stage["p1"](0, 1)
            stage["q1"](0, 1)
            with act.Fori(0, NB) as i:
                act.wait_ge(s_pv, PRIMED + i * NI * KTS)
                for p in range(LEAD):
                    for kind, a, d in HOOKS.get(("lead", p), []):
                        if kind in stage:
                            first[0] = 0
                            with only(act, i, d):
                                stage[kind](pair(i, d), a)
                max_turned(i, 0)
                max_rows(i, 0)
                for l in range(NI):
                    for g in range(NG):
                        gi = l * NG + g
                        for s in range(STEPS):
                            u = gi * STEPS + s
                            kt = gi * TT + s // HG
                            act.wait_ge(s_sT, PRIMED + i * NI * UNITS + u + 1)
                            if s % HG == 0 and kt >= PROB_SLOTS:
                                act.wait_ge(s_pv, PRIMED + i * NI * KTS + kt - PROB_SLOTS + 1)
                            nc.scalar.activation(prob[:, kt % PROB_SLOTS, s % HG, :], score_bank("unit", u),
                                                 ACT.Exp, scale=SC).then_inc(s_exp, 1)
                            if s == AT_COPY and gi > 0:
                                copy_values(i, gi - 1)
                            if s == AT_MAX and gi + 1 < NI * NG:
                                max_turned(i, gi + 1)
                            if s == AT_ROWS and gi + 1 < NI * NG:
                                max_rows(i, gi + 1)
                            for kind, a, d in HOOKS.get((l, g, s), []):
                                if kind in stage:
                                    first[0] = slots_after(u)
                                    with only(act, i, d):
                                        stage[kind](pair(i, d), a)
                copy_values(i, NI * NG - 1)
            first[0] = 0
            for kind, a in END:
                if kind in stage:
                    stage[kind](NB - 1, a)

        @block.vector
        def _(dve):
            k = [0]
            chain = [None, 0]

            def enter(kind, n):
                before = k[0], *chain
                chain[:] = s_dve[kind], n * LINKS[kind]
                k[0] = 0
                return before

            def leave(kind, before):
                assert k[0] == LINKS[kind], (kind, k[0])
                k[0], chain[0], chain[1] = before

            def link(ins):
                mark(ins)
                until(k[0])

            def mark(ins):
                k[0] += 1
                ins.then_inc(chain[0], 1)
                return k[0]

            def until(n):
                dve.wait_ge(chain[0], PRIMED + chain[1] + n)

            V = nc.vector
            first = [0]

            V.memset(ps[:, 6, :], 0.0).then_inc(s_ini, 1)
            V.memset(vp[0][:, :, :, DH:VM], 1.0).then_inc(s_ini, 1)
            V.memset(vp[1][:, :, :, DH:VM], 1.0).then_inc(s_ini, 1)
            for e in range(EPG):
                V.memset(rank0[:, :, :, e:e + 1], float(e)).then_inc(s_ini, 1)

            def setup():
                for j in range(3):
                    dve.wait_ge(s_wt, j + 1)
                    w_ = ps[:, 2 + j, :].rearrange("p (c n) -> p c n", c=CT)
                    if j == 2:
                        V.tensor_copy(wT[:, j], w_).then_inc(s_wtd, 1)
                        continue
                    for c in range(CT):
                        V.tensor_copy(wT[:, j, c].rearrange("p (d h) -> p d h", h=NH),
                                      w_[:, c].rearrange("p (h d) -> p d h", h=NH)).then_inc(s_wtd, 1)
                dve.wait_ge(s_ws, 16 * N_SMALL)
                dve.wait_ge(s_tg, 1)
                V.tensor_scalar(n2_bc[:], n2_bc[:], tg[:, 1:2], None, ALU.mult).then_inc(s_ini, 1)
                for w_, raw in [(fq[:, c_, :], hT[:, 0, c_ * D:(c_ + 1) * D]) for c_ in range(CT)] + [(fkv[0:DC, :], hT[0:DC, 1, 0:D])]:
                    for f in range(2):
                        V.tensor_copy(w_[:, f * P:(f + 1) * P].rearrange("p (j h) -> p j h", h=NH),
                                      raw.rearrange("p (h j f) -> p f j h", f=2, j=DH // 2)[:, f]).then_inc(s_ini, 1)
                dve.wait_ge(s_ini, 3 + EPG + 1 + 6)
                dve.sem_inc(s_set, 1)

            def statistics(i, kind, a, t):
                dve.wait_ge(s_ny[kind], PRIMED + 2 * i + a)
                for tt in range(TT):
                    mark(V.bn_stats(bst[:, NORMS.index(kind), tt, :], t[:, tt, :]))
                until(k[0])
                dve.sem_inc(s_bst[kind], 1)

            def scaled(i, kind, a, dst, t, w):
                e = 2 * NORMS.index(kind) + a
                dve.wait_ge(s_ny[kind], PRIMED + 2 * i + a + 1)
                for tt in range(TT):
                    mark(V.scalar_tensor_tensor(out=dst[:, tt, :], in0=t[:, tt, :], scalar=scale_[:, e, tt:tt + 1], in1=w[:],
                                                op0=ALU.mult, op1=ALU.mult))
                until(k[0])

            def rest_of(n, X):
                dve.wait_ge(s_p0[X], PRIMED + n + 1)
                link(V.tensor_tensor(qk[X][:], qk[X][:], parts[X][:, 0], ALU.subtract))
                dve.sem_inc(s_r0[X], 1)

            def later_parts(X):
                link(V.tensor_copy(parts[X][:, 1], qk[X][:]))
                dve.sem_inc(s_p1[X], 1)
                link(V.tensor_tensor(parts[X][:, 2], qk[X][:], parts[X][:, 1], ALU.subtract))
                dve.sem_inc(s_spl[X], 1)

            def ready(s):
                until(k[0])
                dve.sem_inc(s, 1)

            class Tiles:

                def __init__(self, kind, n):
                    self.kind, self.full, self.own = kind, n * len(OWNER[kind]), n * emptied(kind, "V", 99)
                    self.j = 0

                def next(self):
                    self.j = OWNER[self.kind].index("V", self.j) + 1
                    dve.wait_ge(s_mt[self.kind], PRIMED + self.full + self.j)
                    return misc_bank(first[0], self.j - 1)

                def emptied(self, t):
                    dve.wait_ge(s_mf[self.kind], PRIMED + self.own + emptied(self.kind, "V", t))

            def stage_p1(i, a):
                T = Tiles("p1", 2 * i + a)
                rest_of(i * NI + a, 1)
                if a:
                    dve.wait_ge(s_pv, PRIMED + i * NI * KTS)
                elif not isinstance(i, int):
                    dve.wait_ge(s_pv, PRIMED + i * NI * KTS - KTS)
                for h in range(TT // 2):
                    v = T.next().rearrange("p (t h d) -> p t h d", t=2, h=NH)
                    for t in range(2):
                        ins = V.tensor_tensor(vp[a][:, 2 * h + t, :, 0:DH], v[:, t],
                                              bv_bc[:].rearrange("p (h d) -> p h d", h=NH), ALU.add)
                        ins.then_inc(s_mf["p1"] if t else chain[0], 1)
                    k[0] += 1
                T.emptied(T.j)
                ready(s_vp)

            def stage_p2(i, a):
                T = Tiles("p2", 2 * i + a)
                l = 2 + a
                dve.wait_ge(s_w, 16 * N_LARGE)

                def rotate(X):
                    dve.wait_ge(s_spl[X], PRIMED + i * NI + l)
                    e = T.next()
                    mark(V.tensor_tensor(qk[X][:, 0, :], e, rope_sb[:, 0, :], ALU.mult))
                    V.tensor_tensor(qk[X][:, 1, :], e, rope_sb[:, 1, :], ALU.mult).then_inc(s_mf["p2"], 1)
                    o = T.next()
                    mark(V.scalar_tensor_tensor(out=rb[X][:, 0, :], in0=o, scalar=-1.0, in1=rope_sb[:, 1, :],
                                                op0=ALU.mult, op1=ALU.mult))
                    V.tensor_tensor(rb[X][:, 1, :], o, rope_sb[:, 0, :], ALU.mult).then_inc(s_mf["p2"], 1)
                    until(k[0])
                    T.emptied(T.j)
                    link(V.tensor_tensor(qk[X][:], qk[X][:], rb[X], ALU.add))
                    dve.wait_ge(s_scr[X], PRIMED + (i * NI + l) * SCR[X])
                    link(V.tensor_copy(parts[X][:, 0], qk[X][:]))
                    dve.sem_inc(s_p0[X], 1)

                rotate(0)
                rotate(1)
                rest_of(i * NI + l, 1)

            ee = ez[:, :, NGRP:NR].rearrange("p t (g e) -> p t g e", g=NGRP)

            def route_logits(i, a, T):
                logits = T.next()[:, 0:TT * 16].rearrange("p (t n) -> p t n", t=TT)[:, :, 0:NR]
                V.tensor_tensor(lg[:], logits, gb_bc[:].unsqueeze(1).to_broadcast([P, TT, NR]), ALU.add).then_inc(s_mf["fb"], 1)
                T.emptied(3)
                el = lg[:, :, NGRP:NR].rearrange("p t (g e) -> p t g e", g=NGRP)
                mark(V.tensor_tensor(gmx[:], lg[:, :, 0:1], lg[:, :, 1:2], ALU.max))
                link(V.tensor_reduce(emx[:], el, AX.X, ALU.max))
                mark(V.tensor_tensor(zr[:, :, 0:NGRP], lg[:, :, 0:NGRP], gmx[:].to_broadcast([P, TT, NGRP]), ALU.subtract))
                mark(V.tensor_tensor(zr[:, :, NGRP:NR].rearrange("p t (g e) -> p t g e", g=NGRP), el,
                                     emx[:].unsqueeze(3).to_broadcast([P, TT, NGRP, EPG]), ALU.subtract))
                ready(s_zr)

            def route_group(i, a):
                dve.wait_ge(s_ez, PRIMED + i * 2 + a + 1)
                mark(V.tensor_reduce(esum[:], ee, AX.X, ALU.add))
                mark(V.tensor_tensor(gsum[:], ez[:, :, 0:1], ez[:, :, 1:2], ALU.add))
                mark(V.tensor_tensor(gtop[:], ez[:, :, 0:1], ez[:, :, 1:2], ALU.max))
                mark(V.tensor_tensor(gsel[:, :, 1:2], ez[:, :, 1:2], ez[:, :, 0:1], ALU.is_gt))
                link(V.tensor_copy(rank[:], rank0[:]))
                mark(V.reciprocal(esum[:], esum[:]))
                mark(V.reciprocal(gsum[:], gsum[:]))
                link(V.tensor_scalar(gsel[:, :, 0:1], gsel[:, :, 1:2], -1.0, 1.0, ALU.mult, ALU.add))
                mark(V.tensor_tensor(gtop[:], gtop[:], gsum[:], ALU.mult))
                link(V.tensor_tensor(gsel[:], gsel[:], esum[:], ALU.mult))
                link(V.tensor_tensor(gsel[:], gsel[:], gtop[:].to_broadcast([P, TT, NGRP]), ALU.mult))

            def route_rank(d):
                link(V.tensor_tensor(cmp[:, :, :, 0:EPG - d], ee[:, :, :, d:EPG], ee[:, :, :, 0:EPG - d], ALU.is_gt))
                link(V.tensor_tensor(rank[:, :, :, 0:EPG - d], rank[:, :, :, 0:EPG - d], cmp[:, :, :, 0:EPG - d], ALU.add))
                link(V.tensor_tensor(rank[:, :, :, d:EPG], rank[:, :, :, d:EPG], cmp[:, :, :, 0:EPG - d], ALU.subtract))

            def route_weights():
                link(V.tensor_scalar(rank[:], rank[:], 1.5, None, ALU.is_lt))
                link(V.tensor_tensor(rank[:], rank[:], ee, ALU.mult))
                link(V.tensor_tensor(we[:], rank[:], gsel[:].unsqueeze(3).to_broadcast([P, TT, NGRP, EPG]), ALU.mult))

            def stage_fa(i, a):
                T = Tiles("fa", 2 * i + a)
                y = src[a]
                for h in range(TT // 2):
                    yy = y[:, 2 * h:2 * h + 2, :]
                    V.tensor_tensor(yy, yy, T.next().rearrange("p (t n) -> p t n", t=2), ALU.add).then_inc(s_mf["fa"], 1)
                T.emptied(T.j)
                statistics(i, "y", a, y)

            def norm_y(i, a):
                scaled(i, "y", a, src[a], src[a], n1_bc)
                dve.sem_inc(s_xr, 1)

            def stage_fb(i, a):
                T = Tiles("fb", 2 * i + a)
                y = src[a]
                route_logits(i, a, T)
                for net in range(2):
                    for n in range(HT):
                        nth = net * HT + n
                        dve.wait_ge(s_th, PRIMED + (2 * i + a) * 2 * HT + nth + 1)
                        if nth >= 2:
                            T.emptied(T.j)
                        V.scalar_tensor_tensor(out=uu[:, nth % 2, :], in0=th[:, nth % 2, :], scalar=1.0, in1=T.next(),
                                               op0=ALU.add, op1=ALU.mult).then_inc(s_mf["fb"], 1)
                        T.emptied(T.j)
                        V.scalar_tensor_tensor(out=hT[:, n, :], in0=uu[:, nth % 2, :], scalar=0.5, in1=T.next(),
                                               op0=ALU.mult, op1=ALU.mult).then_inc(s_mf["fb"], 1)
                        if nth == 0:
                            route_group(i, a)
                        elif nth < EPG:
                            route_rank(nth)
                        elif nth == EPG:
                            route_weights()
                    if net == 0:
                        for h in range(TT // 2):
                            yy = y[:, 2 * h:2 * h + 2, :]
                            V.tensor_tensor(yy, yy, T.next().rearrange("p (t n) -> p t n", t=2), ALU.add).then_inc(s_mf["fb"], 1)
                for tt in range(TT):
                    for e in range(0, NE, 2):
                        r = T.next()
                        T.emptied(T.j - 1)
                        link(V.scalar_tensor_tensor(out=y[:, tt, :], in0=r[:, 0:D], scalar=we[:, tt, e // EPG, e % EPG:e % EPG + 1],
                                                    in1=y[:, tt, :], op0=ALU.mult, op1=ALU.add))
                        e += 1
                        V.scalar_tensor_tensor(out=y[:, tt, :], in0=r[:, D:2 * D], scalar=we[:, tt, e // EPG, e % EPG:e % EPG + 1],
                                               in1=y[:, tt, :], op0=ALU.mult, op1=ALU.add).then_inc(s_mf["fb"], 1)
                assert T.j == FB
                T.emptied(T.j)
                statistics(i, "out", a, y)

            def finish(i, a):
                scaled(i, "out", a, sa[a], src[a], n2_bc)
                mark(V.tensor_tensor(sa[a][:], sa[a][:], xin[a][:], ALU.add))
                ready(s_fin)

            def s2(i, a):
                dve.wait_ge(s_x1, PRIMED + i * 2 + a + 1)
                statistics(i, "x1", a, xin[a])

            def n1(i, a):
                dve.wait_ge(s_ldx[a], PRIMED + 16 + i * 16)
                statistics(i, "x", a, xin[a])

            stage = {"s1": n1, "s2": s2, "p1": stage_p1, "p2": stage_p2, "fa": stage_fa, "nf": norm_y, "fb": stage_fb,
                     "no": finish}

            def run(kind, j, a):
                before = enter(kind, 2 * j + a)
                stage[kind](j, a)
                leave(kind, before)

            def row_max(i, l, p):
                q = l * PAIRS + p
                gi = q // (PAIRS // NG)
                h, t2 = p % (PAIRS // NG) // 2, p % 2
                c, bank = ring.take()
                dve.wait_ge(s_rf, PRIMED + i * N_RING + c + 1)
                V.tensor_reduce(negm[:, gi % 2, 2 * t2:2 * t2 + 2, h], ps[:, bank:bank + 2, :], AX.X, ALU.max,
                                negate=True).then_inc(s_re, 1)
                if (p + 1) % (PAIRS // NG) == 0:
                    dve.wait_ge(s_re, PRIMED + i * N_RING + c + 1)
                    m, o = negm[:, gi % 2], m2[:, gi % 2]
                    link(V.tensor_copy(o[:, :, 0, :], m))
                    mark(V.tensor_tensor(o[:, :, 1, :], m, o[:, :, 0, :], ALU.subtract))
                    ready(s_m2)

            def heads_out(i, gi):
                l, g = divmod(gi, NG)
                a = l % 2
                c, bank = ring.take()
                if l < 2 and g == 0:
                    dve.wait_ge(s_st[a], PRIMED + i * 16)
                dve.wait_ge(s_rf, PRIMED + i * N_RING + c + 1)
                o = ps[:, bank, :].rearrange("p (t h d) -> p t h d", t=TT, h=HG)
                link(V.reciprocal(rec[:], o[:, :, :, DH]))
                V.tensor_tensor(sa[a][:, :, g * HG * DH:(g + 1) * HG * DH].rearrange("p t (h d) -> p t h d", h=HG),
                                     o[:, :, :, 0:DH], rec[:].unsqueeze(3).to_broadcast([P, TT, HG, DH]), ALU.mult).then_inc(s_re, 1)
                dve.wait_ge(s_re, PRIMED + i * N_RING + c + 1)
                if l < 2:
                    dve.sem_inc(s_hd, 1)
                elif g == NG - 1:
                    dve.sem_inc(s_sa, 1)

            run("s1", 0, 0)
            setup()
            run("s1", 0, 1)
            before = enter("split q", 0)
            rest_of(0, 0)
            later_parts(0)
            leave("split q", before)
            run("p1", 0, 0)
            before = enter("split k", 0)
            later_parts(1)
            leave("split k", before)
            run("p1", 0, 1)
            with dve.Fori(0, NB) as i:
                before = enter("attention", i)
                ring = Ring()
                for p in range(LEAD):
                    row_max(i, 0, p)
                    for kind, a, d in HOOKS.get(("lead", p), []):
                        if kind in stage:
                            first[0] = 0
                            with only(dve, i, d):
                                run(kind, pair(i, d), a)
                for l in range(NI):
                    for g in range(NG):
                        gi = l * NG + g
                        for s in range(STEPS):
                            if s % 2:
                                p = (g * STEPS + s) // 2 + LEAD
                                if p < PAIRS:
                                    row_max(i, l, p)
                                elif l + 1 < NI:
                                    row_max(i, l + 1, p - PAIRS)
                            if s == AT_HEADS and gi > 0:
                                heads_out(i, gi - 1)
                            for kind, a, d in HOOKS.get((l, g, s), []):
                                if kind in stage:
                                    first[0] = slots_after(gi * STEPS + s)
                                    with only(dve, i, d):
                                        run(kind, pair(i, d), a)
                heads_out(i, NI * NG - 1)
                leave("attention", before)
            first[0] = 0
            for kind, a in END:
                run(kind, NB - 1, a)

        @block.tensor
        def _(pe):
            MM, TR = nc.tensor.matmul, nc.tensor.transpose
            first = [0]
            pe.wait_ge(s_id, 4)
            pe.wait_ge(s_wn, 48)
            for j, w in enumerate((src[0], src[1], sa[0])):
                for c in range(CT):
                    for o in range(CT):
                        last = TR(ps[:, 2 + j, c * D + o * P:c * D + (o + 1) * P], w[:, o, c * P:(c + 1) * P], identf[:])
                last.then_inc(s_wt, 1)

            class Tiles:

                def __init__(self, kind, n, i):
                    self.kind, self.n, self.j, self.i = kind, n, 0, i

                def next(self):
                    if self.j >= 3:
                        self.emptied(self.j - 2)
                    elif first[0] + self.j >= 3:
                        slot_empty(self.i, first[0] + self.j - 3)
                    self.j += 1
                    return misc_bank(first[0], self.j - 1)

                def emptied(self, t):
                    for who, s_ in (("A", s_ma[self.kind]), ("V", s_mf[self.kind])):
                        if emptied(self.kind, who, t):
                            pe.wait_ge(s_, PRIMED + self.n * emptied(self.kind, who, 99) + emptied(self.kind, who, t))

            def turn(T, t):
                for c in range(CT):
                    o = T.next()
                    for tt in range(TT):
                        last = TR(o[:, tt * P:(tt + 1) * P], t[:, tt, c * P:(c + 1) * P], identf[:])
                    last.then_inc(s_mt[T.kind], 1)

            def product(o, terms, T=None, tiles=()):
                for n, (w, r) in enumerate(terms):
                    if n < len(tiles):
                        T.emptied(tiles[n])
                    last = MM(o, w, r, start=(n == 0), stop=(n == len(terms) - 1))
                return last

            def stage_p1(i, a, T):
                pe.wait_ge(s_src, PRIMED + 2 * (i * NI + a + 1))
                turn(T, src[a])
                pe.wait_ge(s_ldc, PRIMED + i * 32 + 16 * (a + 1))
                turn(T, ctxs)
                pe.wait_ge(s_wtd, 2 * CT + 1)
                for X, r in ((0, nT), (1, cT)):
                    for o in range(CT):
                        b_ = T.next()
                        product(b_, [(wT[:, X, k, o * P:(o + 1) * P], r[:, k, :]) for k in range(CT)],
                                T, (1 + 2 * X, 2 + 2 * X)).then_inc(s_mt[T.kind], 1)
                for h in range(TT // 2):
                    o = T.next()
                    for t in range(2):
                        tt = 2 * h + t
                        last = product(o[:, t * D:(t + 1) * D], [(cT[:, k, tt * P:(tt + 1) * P], wT[:, 2, k, :]) for k in range(CT)])
                    last.then_inc(s_mt[T.kind], 1)

            def stage_p2(i, a, T):
                pe.wait_ge(s_w, 16 * N_LARGE)
                pe.wait_ge(s_src, PRIMED + 2 * (i * NI + 2 + a + 1))
                turn(T, src[a])

                def halves(w, r):
                    for f in range(2):
                        o = T.next()
                        product(o, [(w_[:, f * P:(f + 1) * P], r_) for w_, r_ in zip(w, r)],
                                T, [T.j - len(w) + n for n in range(len(w))] if f == 0 else ()).then_inc(s_mt[T.kind], 1)

                halves([fq[:, k, :] for k in range(CT)], [nT[:, k, :] for k in range(CT)])
                product(T.next(), [(fkvc[:, k, :], nT[:, k, :]) for k in range(CT)]).then_inc(s_mt[T.kind], 1)
                halves([fkv[0:DC, :]], [cT[0:DC, 0, :]])
                for h in range(TT // 2):
                    o = T.next()
                    for t in range(2):
                        tt = 2 * h + t
                        last = MM(o[:, t * D:(t + 1) * D], cT[DC:2 * DC, 0, tt * P:(tt + 1) * P], fkv[DC:2 * DC, :],
                                  start=True, stop=True)
                    last.then_inc(s_mt[T.kind], 1)

            def stage_fa(i, a, T):
                pe.wait_ge(s_sa, PRIMED + i * 2 + a + 1)
                turn(T, sa[a])
                for h in range(TT // 2):
                    o = T.next()
                    for t in range(2):
                        tt = 2 * h + t
                        last = product(o[:, t * D:(t + 1) * D], [(nT[:, k, tt * P:(tt + 1) * P], fo[:, k, :]) for k in range(CT)],
                                       T, (1, 2))
                    last.then_inc(s_mt[T.kind], 1)

            def stage_fb(i, a, T):
                pe.wait_ge(s_xr, PRIMED + i * 2 + a + 1)
                pe.wait_ge(s_wl, 16 * N_LATE)
                turn(T, src[a])
                o = T.next()
                for tt in range(TT):
                    last = product(o[:, tt * 16:tt * 16 + NR], [(cT[:, k, tt * P:(tt + 1) * P], fg[:, k, :]) for k in range(CT)],
                                   T, (1, 2))
                last.then_inc(s_mt[T.kind], 1)
                for net in range(2):
                    for j in range(HT):
                        for half in range(2):
                            c = half * HID + j * P
                            product(T.next(), [(fin[:, net, k, c:c + P], cT[:, k, :]) for k in range(CT)]).then_inc(s_mt[T.kind], 1)
                    hidden = [T.j - 2 * (HT - 1 - k) for k in range(HT)]
                    if net == 0:
                        for h in range(TT // 2):
                            o = T.next()
                            for t in range(2):
                                tt = 2 * h + t
                                last = product(o[:, t * D:(t + 1) * D],
                                               [(hT[:, k, tt * P:(tt + 1) * P], fout[:, k, :]) for k in range(HT)], T, hidden)
                            last.then_inc(s_mt[T.kind], 1)
                for tt in range(TT):
                    for e in range(0, NE, 2):
                        o = T.next()
                        product(o, [(hT[:, k, tt * P:(tt + 1) * P], w2[:, k, e:e + 2, :].rearrange("p e n -> p (e n)"))
                                    for k in range(HT)], T, hidden if tt == 0 and e == 0 else ()).then_inc(s_mt[T.kind], 1)
                assert T.j == FB

            stage = {"p1": stage_p1, "p2": stage_p2, "fa": stage_fa, "fb": stage_fb}

            def run(kind, j, a, i=None):
                T = Tiles(kind, 2 * j + a, i)
                stage[kind](j, a, T)
                T.emptied(T.j)

            def ring_bank(i):
                c, bank = ring.take()
                pe.wait_ge(s_re, PRIMED + i * N_RING + max(c - 1, 0))
                return bank

            def score_bank_free(i, kind, n):
                slot = SLOTS.index((kind, n))
                if slot >= 3:
                    slot_empty(i, slot - 3)

            def slot_empty(i, slot):
                kind, n = SLOTS[slot]
                if kind == "unit":
                    pe.wait_ge(s_exp, PRIMED + i * NI * UNITS + n + 1)
                else:
                    pe.wait_ge(s_mts, PRIMED + i * NI * NG + n + 1)

            def max_pair(i, l, p):
                q = l * PAIRS + p
                gi = q // (PAIRS // NG)
                g = gi % NG
                h, t2 = p % (PAIRS // NG) // 2, p % 2
                if p % (PAIRS // NG) == 0:
                    pe.wait_ge(s_stk[g], PRIMED + (i * NI + gi // NG + 1) * 64)
                bank = ring_bank(i)
                for t in range(2):
                    tt = 2 * t2 + t
                    last = MM(ps[:, bank + t, :], qs[0:STK, g, h, tt * P:(tt + 1) * P], ks[0:STK, g, h, :],
                              start=True, stop=True)
                last.then_inc(s_rf, 1)

            def turn_max(i, gi):
                pe.wait_ge(s_m2, PRIMED + i * NI * NG + gi + 1)
                score_bank_free(i, "turned", gi)
                o = score_bank("turned", gi)[:, 0:L // 2].bitcast(BF16)
                for tt in range(TT):
                    last = TR(o[0:MPART * HG, tt * P:(tt + 1) * P],
                              m2[:, gi % 2, tt].rearrange("p s h -> p (s h)"), identb[:])
                last.then_inc(s_mtf, 1)

            def turn_heads(i, gi):
                pe.wait_ge(s_oc, PRIMED + i * NI * NG + gi + 1)
                bank = ring_bank(i)
                for tt in range(TT):
                    last = TR(ps[:, bank, tt * P:(tt + 1) * P], oT[:, tt * P:(tt + 1) * P], identf[:])
                last.then_inc(s_rf, 1)

            def values(i, gi, kt):
                l, g = divmod(gi, NG)
                kk = gi * TT + kt
                if kt == 0:
                    pe.wait_ge(s_oc, PRIMED + i * NI * NG + gi)
                    if g == 0:
                        pe.wait_ge(s_vp, PRIMED + i * NI + l + 1)
                pe.wait_ge(s_exp, PRIMED + i * NI * UNITS + HG * (kk + 1))
                for h in range(HG):
                    last = MM(ps[32 * h:32 * h + VM, 6, :], vp[l % 2][:, kt, g * HG + h, :], prob[:, kk % PROB_SLOTS, h, :],
                              start=(kt == 0), stop=(kt == TT - 1))
                last.then_inc(s_pv, 1)

            run("p1", 0, 0)
            run("p1", 0, 1)
            pe.wait_ge(s_set, 3)
            pe.wait_ge(s_one, 1)
            with pe.Fori(0, NB) as i:
                ring = Ring()
                for p in range(LEAD):
                    if p == PAIRS // NG + 1:
                        turn_max(i, 0)
                    max_pair(i, 0, p)
                    for kind, a, d in HOOKS.get(("lead", p), []):
                        if kind in stage:
                            pe.wait_ge(s_exp, PRIMED + i * NI * UNITS)
                            pe.wait_ge(s_mts, PRIMED + i * NI * NG)
                            first[0] = 0
                            with only(pe, i, d):
                                run(kind, pair(i, d), a)
                for l in range(NI):
                    for g in range(NG):
                        gi = l * NG + g
                        for s in range(STEPS):
                            u = gi * STEPS + s
                            kt, h = divmod(s, HG)
                            if s == 0:
                                pe.wait_ge(s_mrow, PRIMED + (i * NI * NG + gi + 1) * 16 * MPART)
                            score_bank_free(i, "unit", u)
                            MM(score_bank("unit", u), ks[:, g, h, kt * P:(kt + 1) * P], qs[:, g, h, :],
                               start=True, stop=True).then_inc(s_sT, 1)
                            if s % 2:
                                p = (g * STEPS + s) // 2 + LEAD
                                if p < PAIRS:
                                    max_pair(i, l, p)
                                elif l + 1 < NI:
                                    max_pair(i, l + 1, p - PAIRS)
                            if s % HG == HG - 1 and (kt or gi):
                                values(i, *((gi, kt - 1) if kt else (gi - 1, TT - 1)))
                            if s == AT_HEADS and gi > 0:
                                turn_heads(i, gi - 1)
                            if s == AT_MAX and gi + 1 < NI * NG:
                                turn_max(i, gi + 1)
                            for kind, a, d in HOOKS.get((l, g, s), []):
                                if kind in stage:
                                    first[0] = slots_after(u)
                                    with only(pe, i, d):
                                        run(kind, pair(i, d), a, i)
                values(i, NI * NG - 1, TT - 1)
                turn_heads(i, NI * NG - 1)
            pe.wait_ge(s_exp, PRIMED + NB * NI * UNITS)
            pe.wait_ge(s_mts, PRIMED + NB * NI * NG)
            first[0] = 0
            for kind, a in END:
                if kind in stage:
                    run(kind, NB - 1, a)


PRIMED = 64
N_SMALL, N_LARGE, N_LATE = 10, 10, 11
LINKS = {"s1": 4, "s2": 4, "split q": 3, "split k": 2, "p1": 3, "p2": 9, "fa": 4, "nf": 4, "fb": 47, "no": 5, "attention": 48}
POOL_LINKS = {"x": 6, "x1": 6, "y": 7, "out": 7, "split": 3, "add": 2}


def rope_table(L, dh, nh):
    inv = (np.float32(1.0) / np.float32(10000.0) ** (np.arange(0, dh, 2, dtype=np.float32) / np.float32(dh))).astype(np.float32)
    ang = np.arange(L, dtype=np.float32)[:, None] * inv[None, :]
    t = np.stack([np.cos(ang), np.sin(ang)]).astype(np.float32)
    return np.ascontiguousarray(np.repeat(t.transpose(0, 2, 1), nh, axis=1))


_INS = ["x", "ctx_1024", "g_xattn", "g_ffn", "L0_xattn_wq", "L0_xattn_bq", "L0_xattn_wk", "L0_xattn_bk", "L0_xattn_wv",
        "L0_xattn_bv", "L0_ffn_Wq", "L0_ffn_Wk_c", "L0_ffn_Wv_c", "L0_ffn_Wk", "L0_ffn_Wv", "L0_ffn_Wo", "L0_ffn_W_shared_in",
        "L0_ffn_W_shared_out", "L0_ffn_W1_shared", "L0_ffn_W2_experts", "L0_ffn_Wg_gate", "L0_ffn_We_gate",
        "L0_ffn_group_bias", "L0_ffn_expert_bias", "L0_ffn_norm1_w", "L0_ffn_norm2_w"]


def kernel(**inputs):
    import concourse.bacc as _bacc
    from concourse.bass_utils import run_bass_kernel_spmd as _run

    nc = _bacc.Bacc("TRN2", target_bir_lowering=False, num_devices=1)
    arrays, args = {}, []
    given = {name: np.ascontiguousarray(inputs[name]) for name in _INS}
    B, L, D = given["x"].shape
    given["rope"] = rope_table(L, 16, 16)
    for name, a in given.items():
        arrays[f"in_{name}_dram"] = a
        args.append(nc.dram_tensor(f"in_{name}_dram", a.shape, mybir.dt.from_np(a.dtype), kind="ExternalInput").ap())
    args.append(nc.dram_tensor("out_dram", (B, L, D), F32, kind="ExternalOutput").ap())
    flamingo_block(nc, *args)
    r = _run(nc, [arrays], core_ids=[0])
    return r.results[0]["out_dram"]
```
